# Optimizing a Trainium2 kernel written in Bass

```python
import numpy as np
import jax
import jax.numpy as jnp

def _softmax(x, axis=-1):
    return jax.nn.softmax(x, axis=axis)

def _gelu(x):
    return jax.nn.gelu(x, approximate=True)

def _silu(x):
    return jax.nn.silu(x)

def _sigmoid(x):
    return jax.nn.sigmoid(x)

def _layernorm(x, axis=-1, eps=1e-05):
    m = jnp.mean(x, axis=axis, keepdims=True)
    v = jnp.var(x, axis=axis, keepdims=True)
    return (x - m) / jnp.sqrt(v + eps)

def _scatter_add(tgt, idx, src, axis=0):
    return tgt.at[idx].add(src)

def _segment_sum(src, seg, n):
    return jax.ops.segment_sum(src, seg, n)
kernel_name = 'mk_macaron_d1_jaxref_r8_8198d4'

def setup_inputs(seed: int=0):
    np.random.seed(seed)
    _w = jnp.asarray

    def _L0_attn_setup():
        import jax, jax.numpy as jnp
        import numpy as np
        EMBED_DIM = 256
        NUM_HEADS = 32
        NUM_KV_HEADS = 8
        HEAD_DIM = EMBED_DIM // NUM_HEADS
        KV_REPEAT = NUM_HEADS // NUM_KV_HEADS
        ROPE_BASE = 10000.0

        def rotate_half(x):
            x_even = x[..., ::2]
            x_odd = x[..., 1::2]
            return jnp.stack((-x_odd, x_even), axis=-1).reshape(x.shape)

        def rope_cos_sin(seq_len, dtype, start_pos=0):
            inv_freq = 1.0 / ROPE_BASE ** (jnp.arange(0, HEAD_DIM, 2, dtype=jnp.float32) / HEAD_DIM)
            pos = jnp.arange(start_pos, start_pos + seq_len, dtype=jnp.float32)
            freqs = jnp.outer(pos, inv_freq)
            cos = jnp.repeat(jnp.cos(freqs), 2, axis=-1).astype(dtype)
            sin = jnp.repeat(jnp.sin(freqs), 2, axis=-1).astype(dtype)
            return (cos[None, None], sin[None, None])
        key = jax.random.key(seed)
        ks = jax.random.split(key, 5)
        s = 0.02
        x = jax.random.normal(ks[0], (2, 256, EMBED_DIM), dtype=jnp.float32)
        Wq = jax.random.normal(ks[1], (EMBED_DIM, EMBED_DIM), dtype=jnp.float32) * s
        Wk = jax.random.normal(ks[2], (EMBED_DIM, NUM_KV_HEADS * HEAD_DIM), dtype=jnp.float32) * s
        Wv = jax.random.normal(ks[3], (EMBED_DIM, NUM_KV_HEADS * HEAD_DIM), dtype=jnp.float32) * s
        Wo = jax.random.normal(ks[4], (EMBED_DIM, EMBED_DIM), dtype=jnp.float32) * s
        return {'x': x, 'Wq': Wq, 'bq': jnp.zeros((EMBED_DIM,), jnp.float32), 'Wk': Wk, 'bk': jnp.zeros((NUM_KV_HEADS * HEAD_DIM,), jnp.float32), 'Wv': Wv, 'bv': jnp.zeros((NUM_KV_HEADS * HEAD_DIM,), jnp.float32), 'Wo': Wo, 'bo': jnp.zeros((EMBED_DIM,), jnp.float32)}
    _L0_attn_in = _L0_attn_setup()

    def _L0_ffn_setup():
        import jax, jax.numpy as jnp
        import numpy as np

        def _sparsify_2to4(h):
            B, S, I = h.shape
            g = h.reshape(B, S, I // 4, 4)
            a = jnp.abs(g)
            _, idx = jax.lax.top_k(a, 2)
            pos = jnp.arange(4)
            mask = (pos == idx[..., 0:1]) | (pos == idx[..., 1:2])
            return (g * mask.astype(g.dtype)).reshape(B, S, I)
        key = jax.random.key(seed)
        k1, k2, k3, k4 = jax.random.split(key, 4)
        B, S, H, I = (4, 256, 256, 1024)
        x = jax.random.normal(k1, (B, S, H), dtype=jnp.float32)
        w_gate = jax.random.normal(k2, (H, I), dtype=jnp.float32) / np.sqrt(H)
        w_up = jax.random.normal(k3, (H, I), dtype=jnp.float32) / np.sqrt(H)
        w_down = jax.random.normal(k4, (I, H), dtype=jnp.float32) / np.sqrt(I)
        return {'x': x, 'w_gate': w_gate, 'w_up': w_up, 'w_down': w_down}
    _L0_ffn_in = _L0_ffn_setup()
    _d = {'L0_attn_x': _L0_attn_in['x'], 'L0_attn_Wq': _L0_attn_in['Wq'], 'L0_attn_bq': _L0_attn_in['bq'], 'L0_attn_Wk': _L0_attn_in['Wk'], 'L0_attn_bk': _L0_attn_in['bk'], 'L0_attn_Wv': _L0_attn_in['Wv'], 'L0_attn_bv': _L0_attn_in['bv'], 'L0_attn_Wo': _L0_attn_in['Wo'], 'L0_attn_bo': _L0_attn_in['bo'], 'L0_ffn_w_gate': _L0_ffn_in['w_gate'], 'L0_ffn_w_up': _L0_ffn_in['w_up'], 'L0_ffn_w_down': _L0_ffn_in['w_down']}
    _x0 = _d['L0_attn_x']
    _d['L0_attn_x'] = jax.random.normal(jax.random.fold_in(jax.random.key(seed), 1), (2, 1024, 256), dtype=_x0.dtype)
    del _x0
    return _d

def reference(L0_attn_x, L0_attn_Wq, L0_attn_bq, L0_attn_Wk, L0_attn_bk, L0_attn_Wv, L0_attn_bv, L0_attn_Wo, L0_attn_bo, L0_ffn_w_gate, L0_ffn_w_up, L0_ffn_w_down):

    def _L0_attn_ref(x, Wq, bq, Wk, bk, Wv, bv, Wo, bo):
        import jax, jax.numpy as jnp
        import numpy as np
        EMBED_DIM = 256
        NUM_HEADS = 32
        NUM_KV_HEADS = 8
        HEAD_DIM = EMBED_DIM // NUM_HEADS
        KV_REPEAT = NUM_HEADS // NUM_KV_HEADS
        ROPE_BASE = 10000.0

        def rotate_half(x):
            x_even = x[..., ::2]
            x_odd = x[..., 1::2]
            return jnp.stack((-x_odd, x_even), axis=-1).reshape(x.shape)

        def rope_cos_sin(seq_len, dtype, start_pos=0):
            inv_freq = 1.0 / ROPE_BASE ** (jnp.arange(0, HEAD_DIM, 2, dtype=jnp.float32) / HEAD_DIM)
            pos = jnp.arange(start_pos, start_pos + seq_len, dtype=jnp.float32)
            freqs = jnp.outer(pos, inv_freq)
            cos = jnp.repeat(jnp.cos(freqs), 2, axis=-1).astype(dtype)
            sin = jnp.repeat(jnp.sin(freqs), 2, axis=-1).astype(dtype)
            return (cos[None, None], sin[None, None])
        B, T, C = x.shape
        q = (x @ Wq + bq).reshape(B, T, NUM_HEADS, HEAD_DIM).transpose(0, 2, 1, 3)
        k = (x @ Wk + bk).reshape(B, T, NUM_KV_HEADS, HEAD_DIM).transpose(0, 2, 1, 3)
        v = (x @ Wv + bv).reshape(B, T, NUM_KV_HEADS, HEAD_DIM).transpose(0, 2, 1, 3)
        cos, sin = rope_cos_sin(T, q.dtype, start_pos=0)
        q = q * cos + rotate_half(q) * sin
        k = k * cos + rotate_half(k) * sin
        k_rep = jnp.repeat(k, KV_REPEAT, axis=1)
        v_rep = jnp.repeat(v, KV_REPEAT, axis=1)
        scale = np.sqrt(HEAD_DIM).astype(np.float32)
        scores = jnp.einsum('bhqd,bhkd->bhqk', q, k_rep) / scale
        qpos = jnp.arange(T)[:, None]
        kpos = jnp.arange(T)[None, :]
        scores = jnp.where((kpos > qpos)[None, None], -jnp.inf, scores)
        attn = jax.nn.softmax(scores, axis=-1)
        out = jnp.einsum('bhqk,bhkd->bhqd', attn, v_rep)
        out = out.transpose(0, 2, 1, 3).reshape(B, T, C)
        return out @ Wo + bo

    def _L0_ffn_ref(x, w_gate, w_up, w_down):
        import jax, jax.numpy as jnp
        import numpy as np

        def _sparsify_2to4(h):
            B, S, I = h.shape
            g = h.reshape(B, S, I // 4, 4)
            a = jnp.abs(g)
            _, idx = jax.lax.top_k(a, 2)
            pos = jnp.arange(4)
            mask = (pos == idx[..., 0:1]) | (pos == idx[..., 1:2])
            return (g * mask.astype(g.dtype)).reshape(B, S, I)
        h = jax.nn.silu(jnp.einsum('bsh,hi->bsi', x, w_gate)) * jnp.einsum('bsh,hi->bsi', x, w_up)
        h_sparse = _sparsify_2to4(h)
        return jnp.einsum('bsi,ih->bsh', h_sparse, w_down)
    x = L0_attn_x
    x = x + 0.5 * _L0_ffn_ref(_layernorm(x, axis=-1), L0_ffn_w_gate, L0_ffn_w_up, L0_ffn_w_down)
    x = x + _L0_attn_ref(_layernorm(x, axis=-1), L0_attn_Wq, L0_attn_bq, L0_attn_Wk, L0_attn_bk, L0_attn_Wv, L0_attn_bv, L0_attn_Wo, L0_attn_bo)
    x = x + 0.5 * _L0_ffn_ref(_layernorm(x, axis=-1), L0_ffn_w_gate, L0_ffn_w_up, L0_ffn_w_down)
    return x

_drawn_inputs = setup_inputs


def setup_inputs(seed=0):
    import zlib

    import numpy as np

    out = dict(_drawn_inputs(seed))
    spreads = {'L0_attn_bq': (0.0, 0.8),
     'L0_attn_bk': (0.0, 0.8),
     'L0_attn_bv': (0.0, 0.285),
     'L0_attn_bo': (0.0, 0.1)}
    factors = {'L0_attn_Wq': 8.0, 'L0_attn_Wk': 8.0, 'L0_attn_Wv': 5.52}
    for name, (base, spread) in spreads.items():
        noise = np.random.default_rng([zlib.crc32(name.encode()), seed]).standard_normal(out[name].shape)
        drawn = base * np.exp(spread * noise) if base else spread * noise
        out[name] = jnp.asarray(drawn.astype(out[name].dtype))
    for name, factor in factors.items():
        out[name] = (out[name] * factor).astype(out[name].dtype)
    return out
```

```python
import concourse.bass as bass
from concourse import mybir
from contextlib import ExitStack

F32 = mybir.dt.float32
F32R = mybir.dt.float32r
BF16 = mybir.dt.bfloat16
ALU = mybir.AluOpType
ACT = mybir.ActivationFunctionType

P = 128
EPS = 1e-5
ROPE_BASE = 10000.0
MASKED = -1.0e30


class Steps:

    def __init__(self, sem, per_round):
        self.sem, self.per_round, self.n = sem, per_round, 0

    def mark(self, instruction):
        self.n += 1
        return instruction.then_inc(self.sem, 1)

    def value(self, round_index):
        return self.n + self.per_round * round_index


def wait_apart(engine, sem, value, passed):
    engine.wait_ge(sem, value)
    engine.sem_inc(passed, 1)


def make_identity(pool, ident, signal):
    pool.memset(ident[:], 0.0).then_inc(signal, 1)
    pool.wait_ge(signal, 1)
    pool.affine_select(out=ident[:], in_=ident[:], compare_op=ALU.not_equal, fill=1.0, base=0,
                       pattern=[[-1, P]], channel_multiplier=1).then_inc(signal, 1)


class NormedChunks:

    def __init__(self, nc, ctx, tag, x, ident, N):
        _, self.TILES, self.C = x.shape
        self.x, self.ident, self.N = x, ident, N
        self.TPC = N // P
        self.KT = self.C // P
        TPC, C, KT = self.TPC, self.C, self.KT

        def sb(name, shape, dt):
            return ctx.enter_context(nc.sbuf_tensor(f"{tag}_{name}", shape, dt))

        def sem(name):
            return ctx.enter_context(nc.semaphore(f"{tag}_{name}"))

        self.stats = sb("stats", [P, TPC, 6], F32)
        self.mean_var = sb("mean_var", [P, TPC, 2], F32)
        self.var_eps = sb("var_eps", [P, TPC], F32)
        self.rstd = sb("rstd", [P, TPC], F32)
        self.minus_half = sb("minus_half", [P, TPC], F32)
        self.xn = sb("xn", [P, TPC, C], F32)
        self.xt_hi = sb("xt_hi", [P, KT, N], F32R)
        self.xt_lo = sb("xt_lo", [P, KT, N], F32R)
        self.xt_ps = ctx.enter_context(nc.psum_tensor(f"{tag}_xt_ps", [P, KT, N], F32))
        self.passed = sem("passed")
        self.stats_step = sem("stats_step")
        self.stats_ready = sem("stats_ready")
        self.var_ready = sem("var_ready")
        self.rstd_ready = sem("rstd_ready")
        self.xn_ready = sem("xn_ready")
        self.xt_done = sem("xt_done")
        self.hi_ready = sem("xt_hi_ready")
        self.lo_ready = sem("xt_lo_ready")

    def x_tile(self, c, t):
        return self.x[:, bass.ds(c * self.TPC + t, 1), :].rearrange("p a c -> p (a c)")

    def statistics(self, dve, c):
        for t in range(self.TPC):
            dve.bn_stats(self.stats[:, t, :], self.x_tile(c, t)).then_inc(self.stats_step, 1)
        for t in range(self.TPC):
            wait_apart(dve, self.stats_step, c * self.TPC + t + 1, self.passed)
            last = dve.bn_aggr(self.mean_var[:, t, :], self.stats[:, t, :])
        last.then_inc(self.stats_ready, 1)

    def exponents(self, pool):
        pool.memset(self.minus_half[:], -0.5).then_inc(self.var_ready, 1)

    def inverse_deviation(self, pool, c):
        wait_apart(pool, self.stats_ready, c + 1, self.passed)
        pool.tensor_scalar(self.var_eps[:], self.mean_var[:, :, 1], EPS, None, ALU.add).then_inc(self.var_ready, 1)
        pool.wait_ge(self.var_ready, c + 2)
        pool.tensor_tensor(self.rstd[:], self.var_eps[:], self.minus_half[:], ALU.pow).then_inc(self.rstd_ready, 1)

    def normalise(self, dve, c):
        dve.wait_ge(self.rstd_ready, c + 1)
        for t in range(self.TPC):
            last = dve.tensor_scalar(self.xn[:, t, :], self.x_tile(c, t), self.mean_var[:, t, 0:1],
                                     self.rstd[:, t:t + 1], ALU.subtract, ALU.mult)
        last.then_inc(self.xn_ready, 1)

    def transpose(self, pe, c):
        pe.wait_ge(self.xn_ready, c + 1)
        for t in range(self.TPC):
            for k in range(self.KT):
                last = pe.transpose(self.xt_ps[:, k, t * P:(t + 1) * P], self.xn[:, t, k * P:(k + 1) * P],
                                    self.ident[:])
        last.then_inc(self.xt_done, 1)

    def high_parts(self, act, c):
        act.wait_ge(self.xt_done, c + 1)
        act.activation(self.xt_hi[:], self.xt_ps[:], ACT.Copy).then_inc(self.hi_ready, 1)

    def low_parts(self, dve, c):
        dve.wait_ge(self.hi_ready, c + 1)
        dve.tensor_tensor(self.xt_lo[:], self.xt_ps[:], self.xt_hi[:].bitcast(F32), ALU.subtract)\
           .then_inc(self.lo_ready, 1)

    def wait_split(self, pe, c):
        pe.wait_ge(self.hi_ready, c + 1)
        pe.wait_ge(self.lo_ready, c + 1)


def ffn_phase(nc, tag, x, weights, ident, weights_ready, x_ready, out_rows):
    _, TILES, C = x.shape
    KT = C // P
    wg, wu, wd = weights
    BLKS = wd[0].shape[1]
    J = 4
    N = 512
    TPC = N // P
    CHUNKS = TILES // TPC
    assert BLKS == 2 and CHUNKS >= 3

    with ExitStack() as ctx:
        def sb(name, shape, dt):
            return ctx.enter_context(nc.sbuf_tensor(f"{tag}_{name}", shape, dt))

        def pb(name, shape, dt=F32):
            return ctx.enter_context(nc.psum_tensor(f"{tag}_{name}", shape, dt))

        def sem(name):
            return ctx.enter_context(nc.semaphore(f"{tag}_{name}"))

        normed = NormedChunks(nc, ctx, tag, x, ident, N)
        silu = sb("silu", [P, 2, N], F32)
        h = sb("h", [P, J, N], F32)
        a = sb("a", [P, J, N], F32)
        pair_max = sb("pair_max", [P, 2, N], F32)
        pair_min = sb("pair_min", [P, 2, N], F32)
        first_wins = sb("first_wins", [P, 2, N], BF16)
        both_low = sb("both_low", [P, N], BF16)
        both_high = sb("both_high", [P, N], BF16)
        tilt = sb("tilt", [P, N], BF16)
        rank = sb("rank", [P, J, N], BF16)
        hs = sb("hs", [P, J, N], F32)
        hs_hi = sb("hs_hi", [P, BLKS, J, N], F32R)
        hs_lo = sb("hs_lo", [P, BLKS, J, N], F32R)

        gu = [[pb(f"{w}{i}", [P, N]) for w in ("gate", "up")] for i in range(2)]
        y_ps = pb("y_ps", [P, TPC, C])

        gu_done = sem("gu_done")
        silu_ready = sem("silu_ready")
        h_ready = sem("h_ready")
        abs_ready = sem("abs_ready")
        dve_step = sem("dve_step")
        hs_ready = sem("hs_ready")
        hi_ready = sem("hi_ready")
        lo_ready = sem("lo_ready")
        hs_free = sem("hs_free")
        y_done = sem("y_done")
        y_added = sem("y_added")
        stored = sem("stored")

        block = ctx.enter_context(nc.Block())

        @block.tensor
        def _(pe):
            def gate_up(c, blk, first=False):
                if blk == 0:
                    normed.wait_split(pe, c)
                for j in range(J):
                    i = j % 2
                    if not (first and j < 2):
                        pe.wait_ge(h_ready, (c * BLKS + blk) * J + j - 1)
                    for w, ps in zip((wg, wu), gu[i]):
                        n = 0
                        for k in range(KT):
                            for ws, xs in ((w[0], normed.xt_hi), (w[1], normed.xt_hi), (w[0], normed.xt_lo)):
                                last = pe.matmul(ps[:], ws[:, k, blk, j, :], xs[:, k, :],
                                                 start=(n == 0), stop=(n == 3 * KT - 1))
                                n += 1
                    last.then_inc(gu_done, 1)

            def down(c, blk):
                if blk == 0:
                    pe.wait_ge(y_added, c)
                for j in range(J):
                    n = (c * BLKS + blk) * J + j + 1
                    pe.wait_ge(hi_ready, n)
                    pe.wait_ge(lo_ready, n)
                    for t in range(TPC):
                        rows = slice(t * P, (t + 1) * P)
                        for m, (hp, wp) in enumerate(((hs_hi, wd[0]), (hs_hi, wd[1]), (hs_lo, wd[0]))):
                            last = pe.matmul(y_ps[:, t, :], hp[:, blk, j, rows], wp[:, blk, j, :],
                                             start=(blk == 0 and j == 0 and m == 0 and t % 2 == 0),
                                             stop=(blk == BLKS - 1 and j == J - 1 and m == 2),
                                             skip_group_check=True)
                last.then_inc(hs_free, 1)
                if blk == BLKS - 1:
                    pe.drain().then_inc(y_done, 1)

            pe.sem_inc(hs_free, BLKS)
            pe.wait_ge(weights_ready, 1)
            normed.transpose(pe, 0)
            gate_up(0, 0, first=True)
            with pe.Fori(0, CHUNKS - 1) as c:
                gate_up(c, 1)
                normed.transpose(pe, c + 1)
                down(c, 0)
                gate_up(c + 1, 0)
                down(c, 1)
            gate_up(CHUNKS - 1, 1)
            down(CHUNKS - 1, 0)
            down(CHUNKS - 1, 1)

        @block.scalar
        def _(act):
            def silu_of(c, blk, j):
                n = (c * BLKS + blk) * J + j
                act.wait_ge(gu_done, n + 1)
                act.activation(silu[:, j % 2, :], gu[j % 2][0][:], ACT.Silu).then_inc(silu_ready, 1)

            def abs_of(c, blk, j):
                act.wait_ge(h_ready, (c * BLKS + blk) * J + j + 1)
                act.activation(a[:, j, :], h[:, j, :], ACT.Abs).then_inc(abs_ready, 1)

            def hidden(c, blk):
                for j in range(J):
                    silu_of(c, blk, j)
                    if j:
                        abs_of(c, blk, j - 1)
                abs_of(c, blk, J - 1)

            def high_parts(c, blk):
                act.wait_ge(hs_free, c * BLKS + blk + 1)
                for j in range(J):
                    act.wait_ge(hs_ready, (c * BLKS + blk) * J + j + 1)
                    act.activation(hs_hi[:, blk, j, :], hs[:, j, :], ACT.Copy).then_inc(hi_ready, 1)

            normed.high_parts(act, 0)
            with act.Fori(0, CHUNKS - 1) as c:
                hidden(c, 0)
                high_parts(c, 0)
                hidden(c, 1)
                normed.high_parts(act, c + 1)
                high_parts(c, 1)
            hidden(CHUNKS - 1, 0)
            high_parts(CHUNKS - 1, 0)
            hidden(CHUNKS - 1, 1)
            high_parts(CHUNKS - 1, 1)

        @block.vector
        def _(dve):
            step = Steps(dve_step, per_round=BLKS * 10)

            def hidden(c, blk):
                for j in range(J):
                    dve.wait_ge(silu_ready, (c * BLKS + blk) * J + j + 1)
                    dve.tensor_tensor(h[:, j, :], gu[j % 2][1][:], silu[:, j % 2, :], ALU.mult).then_inc(h_ready, 1)

            def sparsify(c, blk):
                dve.wait_ge(abs_ready, (c * BLKS + blk + 1) * J)
                step.mark(dve.tensor_tensor(pair_max[:], a[:, 0::2, :], a[:, 1::2, :], ALU.max))
                step.mark(dve.tensor_tensor(pair_min[:], a[:, 0::2, :], a[:, 1::2, :], ALU.min))
                step.mark(dve.tensor_tensor(first_wins[:], a[:, 0::2, :], a[:, 1::2, :], ALU.is_ge))
                dve.wait_ge(dve_step, step.value(c) - 1)
                step.mark(dve.tensor_tensor(both_low[:], pair_min[:, 0, :], pair_max[:, 1, :], ALU.is_ge))
                step.mark(dve.tensor_tensor(both_high[:], pair_min[:, 1, :], pair_max[:, 0, :], ALU.is_gt))
                dve.wait_ge(dve_step, step.value(c))
                step.mark(dve.tensor_tensor(tilt[:], both_low[:], both_high[:], ALU.subtract))
                dve.wait_ge(dve_step, step.value(c))
                for j, op in enumerate((ALU.add, ALU.subtract, ALU.subtract, ALU.add)):
                    step.mark(dve.tensor_tensor(rank[:, j, :], first_wins[:, j // 2, :], tilt[:], op))
                at = step.value(c)
                dve.wait_ge(hi_ready, (c * BLKS + blk) * J)
                dve.wait_ge(lo_ready, (c * BLKS + blk) * J)
                for j, (op, bound) in enumerate(((ALU.is_ge, 1.0), (ALU.is_le, 0.0), (ALU.is_ge, 1.0), (ALU.is_le, 0.0))):
                    dve.wait_ge(dve_step, at - 3 + j)
                    dve.scalar_tensor_tensor(out=hs[:, j, :], in0=rank[:, j, :], scalar=bound, in1=h[:, j, :],
                                             op0=op, op1=ALU.mult).then_inc(hs_ready, 1)

            def add_down(c):
                dve.wait_ge(y_done, c + 1)
                rows = x[:, bass.ds(c * TPC, TPC), :].rearrange("p t c -> p (t c)")
                dve.scalar_tensor_tensor(out=rows, in0=y_ps[:].rearrange("p t c -> p (t c)"), scalar=0.5, in1=rows,
                                         op0=ALU.mult, op1=ALU.add).then_inc(y_added, 1)

            def chunk(c, first=False, last=False):
                step.n = 0
                if not last:
                    normed.statistics(dve, c + 1)
                hidden(c, 0)
                sparsify(c, 0)
                if not first:
                    add_down(c - 1)
                if not last:
                    normed.normalise(dve, c + 1)
                hidden(c, 1)
                if not last:
                    normed.low_parts(dve, c + 1)
                sparsify(c, 1)
                assert last or step.n == step.per_round

            dve.wait_ge(x_ready, 16)
            normed.statistics(dve, 0)
            normed.normalise(dve, 0)
            normed.low_parts(dve, 0)
            chunk(0, first=True)
            with dve.Fori(1, CHUNKS - 1) as c:
                chunk(c)
            chunk(CHUNKS - 1, last=True)
            add_down(CHUNKS - 1)

        @block.gpsimd
        def _(pool):
            def low_parts(c, blk):
                pool.wait_ge(hs_free, c * BLKS + blk + 1)
                for j in range(J):
                    pool.wait_ge(hi_ready, (c * BLKS + blk) * J + j + 1)
                    pool.tensor_tensor(hs_lo[:, blk, j, :], hs[:, j, :], hs_hi[:, blk, j, :].bitcast(F32),
                                       ALU.subtract).then_inc(lo_ready, 1)

            normed.exponents(pool)
            normed.inverse_deviation(pool, 0)
            with pool.Fori(0, CHUNKS - 1) as c:
                normed.inverse_deviation(pool, c + 1)
                low_parts(c, 0)
                low_parts(c, 1)
            low_parts(CHUNKS - 1, 0)
            low_parts(CHUNKS - 1, 1)

        @block.sync
        def _(sp):
            if out_rows is not None:
                with sp.Fori(0, CHUNKS) as c:
                    sp.wait_ge(y_added, c + 1)
                    sp.dma_start(out_rows[:, bass.ds(c * TPC, TPC), :],
                                 x[:, bass.ds(c * TPC, TPC), :]).then_inc(stored, 16)
                sp.wait_ge(stored, CHUNKS * 16)
            else:
                sp.wait_ge(y_added, CHUNKS)


def qkv_phase(nc, x, ident, wqkv, bias_cols, bv_row, cos_t, sin_t, q_rows, k_rows, v):
    w_hi, w_lo = wqkv
    N = 512
    B_T = x.shape[1] * P
    CHUNKS = B_T // N
    QM = 2
    UNITS = QM + 1
    _, KVH, _, HD = v.shape
    KV = KVH * HD

    with ExitStack() as ctx:
        def sb(name, shape, dt):
            return ctx.enter_context(nc.sbuf_tensor(f"qkv_{name}", shape, dt))

        def pb(name, shape, dt=F32):
            return ctx.enter_context(nc.psum_tensor(f"qkv_{name}", shape, dt))

        def sem(name):
            return ctx.enter_context(nc.semaphore(f"qkv_{name}"))

        normed = NormedChunks(nc, ctx, "qkv", x, ident, N)
        TPC, KT = normed.TPC, normed.KT
        biases = sb("biases", [P, 2 * UNITS], F32)
        bv = sb("bv", [P, KV], F32)
        cos = sb("cos", [P, B_T], F32)
        sin = sb("sin", [P, B_T], F32)
        by_cos = sb("by_cos", [P, UNITS, N], F32)
        by_sin = sb("by_sin", [P, UNITS, N], F32)
        turned = sb("turned", [P, UNITS, N], F32)
        rest = sb("rest", [P, UNITS, N], F32)
        parts = sb("parts", [P, UNITS, 3, N], BF16)
        qk_ps = [[pb(f"{w}{i}", [P, N]) for w in ("plain", "swapped")] for i in range(2)]
        v_ps = pb("v_ps", [P, TPC, KV])

        tables_loaded = sem("tables_loaded")
        qk_done = sem("qk_done")
        v_done = sem("v_done")
        by_ready = sem("by_ready")
        turned_ready = sem("turned_ready")
        hi_ready = sem("hi_ready")
        rest_ready = sem("rest_ready")
        mid_ready = sem("mid_ready")
        lo_ready = sem("lo_ready")
        v_ready = sem("v_ready")
        stored = [sem(f"stored{u}") for u in range(UNITS)]
        Q_DMAS, K_DMAS = 3, 4

        block = ctx.enter_context(nc.Block())

        @block.tensor
        def _(pe):
            def units(c, first=False):
                normed.wait_split(pe, c)
                for u in range(UNITS):
                    if not (first and u < 2):
                        pe.wait_ge(by_ready, c * UNITS + (0, -1, 1)[u])
                    for which in range(2):
                        col = (2 * u + which) * P
                        n = 0
                        for k in range(KT):
                            for ws, xs in ((w_hi, normed.xt_hi), (w_lo, normed.xt_hi), (w_hi, normed.xt_lo)):
                                last = pe.matmul(qk_ps[u % 2][which][:], ws[:, k, col:col + P], xs[:, k, :],
                                                 start=(n == 0), stop=(n == 3 * KT - 1))
                                n += 1
                    last.then_inc(qk_done, 1)

            def values(c):
                pe.wait_ge(v_ready, c)
                col = 2 * UNITS * P
                for t in range(TPC):
                    rows = slice(t * P, (t + 1) * P)
                    n = 0
                    for k in range(KT):
                        for ws, xs in ((w_hi, normed.xt_hi), (w_lo, normed.xt_hi), (w_hi, normed.xt_lo)):
                            last = pe.matmul(v_ps[:, t, :], xs[:, k, rows], ws[:, k, col:col + KV],
                                             start=(n == 0 and t == 0), stop=(n == 3 * KT - 1), skip_group_check=True)
                            n += 1
                last.then_inc(v_done, 1)

            normed.transpose(pe, 0)
            units(0, first=True)
            values(0)
            with pe.Fori(1, CHUNKS) as c:
                normed.transpose(pe, c)
                units(c)
                values(c)

        @block.scalar
        def _(act):
            def part(c, u, i):
                n = c * UNITS + u
                if i == 0:
                    act.wait_ge(turned_ready, n + 1)
                    act.wait_ge(stored[u], 16 * (Q_DMAS if u < QM else K_DMAS) * c)
                    act.activation(parts[:, u, 0, :], turned[:, u, :], ACT.Copy).then_inc(hi_ready, 1)
                else:
                    act.wait_ge(rest_ready, n + 1)
                    act.activation(parts[:, u, 1, :], rest[:, u, :], ACT.Copy).then_inc(mid_ready, 1)

            with act.Fori(0, CHUNKS) as c:
                normed.high_parts(act, c)
                for u, i in ((0, 0), (1, 0), (0, 1), (2, 0), (1, 1), (2, 1)):
                    part(c, u, i)

        @block.vector
        def _(dve):
            def turn(c, u):
                n = c * UNITS + u
                dve.wait_ge(qk_done, n + 1)
                tokens = bass.ds(c * N, N)
                dve.scalar_tensor_tensor(out=by_cos[:, u, :], in0=qk_ps[u % 2][0][:], scalar=biases[:, 2 * u:2 * u + 1],
                                         in1=cos[:, tokens], op0=ALU.add, op1=ALU.mult)
                dve.scalar_tensor_tensor(out=by_sin[:, u, :], in0=qk_ps[u % 2][1][:],
                                         scalar=biases[:, 2 * u + 1:2 * u + 2], in1=sin[:, tokens],
                                         op0=ALU.add, op1=ALU.mult).then_inc(by_ready, 1)

            def lo_part(c, u):
                dve.wait_ge(mid_ready, c * UNITS + u + 1)
                dve.tensor_tensor(parts[:, u, 2, :], rest[:, u, :], parts[:, u, 1, :], ALU.subtract).then_inc(lo_ready, 1)

            def values(c):
                dve.wait_ge(v_done, c + 1)
                for h in range(KVH):
                    cols = slice(h * HD, (h + 1) * HD)
                    last = dve.tensor_tensor(v[:, h, bass.ds(c * TPC, TPC), :], v_ps[:, :, cols],
                                             bv[:, None, cols].to_broadcast([P, TPC, HD]), ALU.add)
                last.then_inc(v_ready, 1)

            def chunk(c, last=False):
                normed.low_parts(dve, c)
                turn(c, 0)
                turn(c, 1)
                lo_part(c, 0)
                if not last:
                    normed.statistics(dve, c + 1)
                turn(c, 2)
                lo_part(c, 1)
                if not last:
                    normed.normalise(dve, c + 1)
                values(c)
                lo_part(c, 2)

            normed.statistics(dve, 0)
            normed.normalise(dve, 0)
            dve.wait_ge(tables_loaded, 4 * 16)
            with dve.Fori(0, CHUNKS - 1) as c:
                chunk(c)
            chunk(CHUNKS - 1, last=True)

        @block.gpsimd
        def _(pool):
            def add_turned(c, u):
                pool.wait_ge(by_ready, c * UNITS + u + 1)
                pool.tensor_tensor(turned[:, u, :], by_cos[:, u, :], by_sin[:, u, :], ALU.add).then_inc(turned_ready, 1)

            def leave_rest(c, u):
                pool.wait_ge(hi_ready, c * UNITS + u + 1)
                pool.tensor_tensor(rest[:, u, :], turned[:, u, :], parts[:, u, 0, :], ALU.subtract).then_inc(rest_ready, 1)

            def chunk(c, last=False):
                add_turned(c, 0)
                add_turned(c, 1)
                leave_rest(c, 0)
                if not last:
                    normed.inverse_deviation(pool, c + 1)
                add_turned(c, 2)
                leave_rest(c, 1)
                leave_rest(c, 2)

            normed.exponents(pool)
            normed.inverse_deviation(pool, 0)
            with pool.Fori(0, CHUNKS - 1) as c:
                chunk(c)
            chunk(CHUNKS - 1, last=True)

        @block.sync
        def _(sp):
            sp.dma_start(biases[:], bias_cols).then_inc(tables_loaded, 16)
            sp.dma_start(bv[:], bv_row.partition_broadcast(P)).then_inc(tables_loaded, 16)
            sp.dma_start(cos[:], cos_t).then_inc(tables_loaded, 16)
            sp.dma_start(sin[:], sin_t).then_inc(tables_loaded, 16)
            q_places = ((0, 1, 3),), ((3, 1, 2),), ((5, 1, 1),)
            k_places = ((0, 3, 2), (5, 1, 1)), ((1, 3, 2),), ((2, 1, 1),)
            with sp.Fori(0, CHUNKS) as c:
                tokens = bass.ds(c * N, N)
                for u in range(UNITS):
                    rows = q_rows[u * P:(u + 1) * P] if u < QM else k_rows
                    for part, ready in enumerate((hi_ready, mid_ready, lo_ready)):
                        sp.wait_ge(ready, c * UNITS + u + 1)
                        for r0, step, times in (q_places if u < QM else k_places)[part]:
                            src = parts[:rows.shape[0], u, part, :]
                            sp.dma_start(rows[:, r0:r0 + step * (times - 1) + 1:step, tokens],
                                         src[:, None, :].to_broadcast([rows.shape[0], times, N])).then_inc(stored[u], 16)
            for u in range(UNITS):
                sp.wait_ge(stored[u], 16 * (Q_DMAS if u < QM else K_DMAS) * CHUNKS)
            sp.wait_ge(v_ready, CHUNKS)


def attention_phase(nc, q_rows, k_rows, v, heads_out, ident_bf, x, bo_row, T, HD):
    SPLIT = q_rows.shape[1]
    ROWS = SPLIT * HD
    SHIFT = 3
    HEADS = q_rows.shape[0] // HD
    KVH = k_rows.shape[0] // HD
    B = q_rows.shape[2] // T
    GROUPS = B * KVH
    QPK = HEADS // KVH
    KB = T // P
    N = 512
    QC = T // N
    TPC = N // P
    HALF = P // 2
    SCALE = 1.0 / float(HD) ** 0.5
    assert QPK == 4 and QC == 2 and GROUPS % 2 == 0 and ROWS + SHIFT <= HALF

    S_UNITS = [(qc, kb, max(0, kb * P - qc * N)) for qc in range(QC) for kb in range(TPC * (qc + 1))]
    SU = len(S_UNITS)
    DIAGONAL = [u for u, (qc, kb, _) in enumerate(S_UNITS) if kb >= TPC * qc]
    CHUNK_FIRST = [[q for q, _, _ in S_UNITS].index(qc) for qc in range(QC)]
    CHUNK_LAST = [first - 1 for first in CHUNK_FIRST[1:]] + [SU - 1]
    M_UNITS = [(t, h, kc, min(N, (t + 1) * P - kc * N)) for t in range(KB) for kc in range(t // TPC + 1)
               for h in range(QPK)]
    MU = len(M_UNITS)
    MU_HALF = TPC * QPK

    SLOTS = 4
    M_AT = [[[] for _ in range(SLOTS)] for _ in range(SU)]
    total = sum(N - q0 for _, _, q0 in S_UNITS)
    m_total = sum(n for *_, n in M_UNITS)
    done = upto = 0
    ahead = list(range(MU))
    for u, (_, _, q0) in enumerate(S_UNITS):
        for slot in range(SLOTS):
            upto += (N - q0) / SLOTS
            while ahead and done < m_total * upto / total:
                m = ahead.pop(0)
                done += M_UNITS[m][3]
                M_AT[u][slot].append(m)
    M_AT[-1][-1] += ahead
    SHIFT_SECOND = 0
    SHIFT_FIRST = next(u for u in range(SU) if any(m >= MU_HALF for slot in M_AT[u] for m in slot)) + 1
    assert SHIFT_SECOND < SHIFT_FIRST < SU - 1

    with ExitStack() as ctx:
        def sb(name, shape, dt):
            return ctx.enter_context(nc.sbuf_tensor(f"att_{name}", shape, dt))

        def pb(name, shape, dt=F32):
            return ctx.enter_context(nc.psum_tensor(f"att_{name}", shape, dt))

        def sem(name):
            return ctx.enter_context(nc.semaphore(f"att_{name}"))

        mq = [sb(f"mq{e}", [P, QPK // 2, T], BF16) for e in range(2)]
        mk = [sb(f"mk{e}", [P, T], BF16) for e in range(2)]
        sq = [sb(f"sq{e}", [P, QPK // 2, T], BF16) for e in range(2)]
        sk = [sb(f"sk{e}", [P, T], BF16) for e in range(2)]
        vs = [sb(f"vs{e}", [P, KB, 32], F32) for e in range(2)]
        probs = [sb(f"probs{e}", [P, QPK, N], F32) for e in range(2)]
        causal = sb("causal", [P, N], F32)
        scratch = [sb(f"scratch{i}", [P, N], BF16) for i in range(2)]
        max_a = sb("max_a", [P, QPK, KB], F32)
        max_b = sb("max_b", [P, QPK, TPC], F32)
        max_ab = sb("max_ab", [P, TPC, QPK], F32)
        left = sb("left", [P, TPC, QPK], F32)
        shift = [sb(f"shift{i}", [P, TPC, QPK, SHIFT], BF16) for i in range(QC)]
        shift_t = [sb(f"shift_t{i}", [QPK * SHIFT, N], BF16) for i in range(QC)]
        bo = sb("bo", [P, x.shape[2]], F32)

        s_ps = [pb(f"s_ps{i}", [P, 2, N]) for i in range(2)]
        m_ps = [pb(f"m_ps{i}", [P, N]) for i in range(2)]
        o_ps = pb("o_ps", [P, N])
        t_ps = pb("t_ps", [QPK * SHIFT, N], BF16)

        masks_ready = sem("masks_ready")
        ones_ready = sem("ones_ready")
        m_loaded = [sem(f"m_loaded{e}") for e in range(2)]
        s_loaded = [sem(f"s_loaded{e}") for e in range(2)]
        shift_loaded = [sem(f"shift_loaded{i}") for i in range(QC)]
        bo_loaded = sem("bo_loaded")
        v_staged = sem("v_staged")
        m_done = sem("m_done")
        m_taken = sem("m_taken")
        max_step = sem("max_step")
        shift_ready = sem("shift_ready")
        t_done = sem("t_done")
        shift_t_ready = sem("shift_t_ready")
        s_done = sem("s_done")
        exp_done = sem("exp_done")
        masked = sem("masked")
        pv_done = sem("pv_done")
        o_taken = sem("o_taken")
        passed = sem("passed")
        x_biased = sem("x_biased")

        block = ctx.enter_context(nc.Block())

        def after(r, e):
            return (r, 1) if e == 0 else (r + 1, 0)

        ROUNDS = GROUPS // 2

        @block.tensor
        def _(pe):
            def m_unit(r, e, m):
                g = 2 * r + e
                t, h, kc, n = M_UNITS[m]
                if m == 0:
                    pe.wait_ge(m_loaded[e], 16 * 4 * (r + 1))
                if not (isinstance(g, int) and g * MU + m < 2):
                    pe.wait_ge(m_taken, g * MU + m - 1)
                rows = slice(HALF * (h % 2), HALF * (h % 2) + ROWS)
                pe.matmul(m_ps[m % 2][:, :n], mq[e][rows, h // 2, t * P:(t + 1) * P],
                          mk[e][rows, kc * N:kc * N + n], start=True, stop=True).then_inc(m_done, 1)

            def transpose_shift(r, e, qc):
                n = QC * (2 * r + e) + qc
                pe.wait_ge(shift_ready, n + 1)
                pe.wait_ge(shift_t_ready, n)
                for t in range(TPC):
                    last = pe.transpose(t_ps[:, t * P:(t + 1) * P],
                                        shift[qc][:, t, :, :].rearrange("p h s -> p (h s)"), ident_bf[:])
                last.then_inc(t_done, 1)

            def s_unit(r, e, u, pair):
                g = 2 * r + e
                n = g * SU + u
                qc, kb, q0 = S_UNITS[u]
                if pair == 0 and u == 0:
                    pe.wait_ge(s_loaded[e], 16 * 4 * (r + 1))
                if pair == 0 and u in CHUNK_FIRST:
                    pe.wait_ge(shift_loaded[qc], 16 * QPK * (g + 1))
                if not (isinstance(n, int) and n == 0):
                    pe.wait_ge(exp_done, 2 * n + pair - 1)
                for half in range(2):
                    rows = slice(HALF * half, HALF * half + ROWS + SHIFT)
                    last = pe.matmul(s_ps[pair][:, half, q0:], sk[e][rows, kb * P:(kb + 1) * P],
                                     sq[e][rows, pair, qc * N + q0:(qc + 1) * N], start=True, stop=True)
                last.then_inc(s_done, 1)

            def value_unit(r, e, u):
                g = 2 * r + e
                qc, kb, q0 = S_UNITS[u]
                n = g * SU + u
                if u == 0:
                    pe.wait_ge(v_staged, g + 1)
                if u in CHUNK_FIRST:
                    pe.wait_ge(o_taken, QC * g + qc)
                pe.wait_ge(exp_done, 2 * n + 2)
                if u in DIAGONAL:
                    pe.wait_ge(masked, g * len(DIAGONAL) + DIAGONAL.index(u) + 1)
                for h in range(QPK):
                    last = pe.matmul(o_ps[32 * h:32 * (h + 1), q0:], vs[e][:, kb, :], probs[u % 2][:, h, q0:],
                                     start=(u in CHUNK_FIRST), stop=(u in CHUNK_LAST))
                last.then_inc(pv_done, 1)

            def group(r, e, last=False):
                r1, e1 = after(r, e)
                for u in range(SU):
                    def maxima(slot):
                        if not last:
                            for m in M_AT[u][slot]:
                                m_unit(r1, e1, m)

                    ru, eu, nu = (r, e, u + 1) if u < SU - 1 else (r1, e1, 0)
                    ahead = u < SU - 1 or not last
                    if ahead:
                        s_unit(ru, eu, nu, 0)
                    maxima(0)
                    if ahead:
                        s_unit(ru, eu, nu, 1)
                    maxima(1)
                    if u == SHIFT_SECOND:
                        transpose_shift(r, e, 1)
                    if u == SHIFT_FIRST and not last:
                        transpose_shift(r1, e1, 0)
                    maxima(2)
                    value_unit(r, e, u)
                    maxima(3)

            pe.sem_inc(pv_done, 2)
            for m in range(MU):
                m_unit(0, 0, m)
                if m == MU_HALF + QPK:
                    transpose_shift(0, 0, 0)
            s_unit(0, 0, 0, 0)
            s_unit(0, 0, 0, 1)
            with pe.Fori(0, ROUNDS - 1) as r:
                group(r, 0)
                group(r, 1)
            group(ROUNDS - 1, 0)
            group(ROUNDS - 1, 1, last=True)

        @block.vector
        def _(dve):
            def m_unit(r, e, m):
                t, h, kc, n = M_UNITS[m]
                wait_apart(dve, m_done, (2 * r + e) * MU + m + 1, passed)
                if kc == t // TPC:
                    dve.tensor_tensor_reduce(out=scratch[m % 2][:, :n], in0=m_ps[m % 2][:, :n], in1=causal[:, N - n:],
                                             scale=1.0, scalar=-3.0e38, op0=ALU.add, op1=ALU.max,
                                             accum_out=max_a[:, h, t:t + 1]).then_inc(m_taken, 1)
                else:
                    dve.tensor_reduce(max_b[:, h, t - TPC:t - TPC + 1], m_ps[m % 2][:, :n], mybir.AxisListType.X,
                                      ALU.max).then_inc(m_taken, 1)

            step = Steps(max_step, per_round=2 * (3 + 4))

            def split_maxima(r, e, qc):
                g = 2 * r + e
                step.n = (3 + 4) * e + 3 * qc
                dve.wait_ge(m_taken, g * MU + (MU if qc else MU_HALF))
                top = max_a[:, :, qc * TPC:(qc + 1) * TPC].rearrange("p h t -> p t h")
                if qc:
                    step.mark(dve.tensor_tensor(max_ab[:], top, max_b[:].rearrange("p h t -> p t h"), ALU.max))
                    dve.wait_ge(max_step, step.value(r))
                    top = max_ab[:]
                step.mark(dve.tensor_scalar(shift[qc][:, :, :, 0], top, -1.0, None, ALU.mult))
                dve.wait_ge(max_step, step.value(r))
                step.mark(dve.scalar_tensor_tensor(out=left[:], in0=top, scalar=-1.0, in1=shift[qc][:, :, :, 0],
                                                   op0=ALU.mult, op1=ALU.subtract))
                dve.wait_ge(max_step, step.value(r))
                step.mark(dve.tensor_copy(shift[qc][:, :, :, 1], left[:]))
                dve.wait_ge(max_step, step.value(r))
                dve.tensor_tensor(shift[qc][:, :, :, 2], left[:], shift[qc][:, :, :, 1], ALU.subtract)\
                   .then_inc(shift_ready, 1)

            def group(r, e):
                for m in range(MU):
                    m_unit(r, e, m)
                    if m == MU_HALF - 1:
                        split_maxima(r, e, 0)
                split_maxima(r, e, 1)

            dve.wait_ge(masks_ready, 2)
            with dve.Fori(0, ROUNDS) as r:
                group(r, 0)
                group(r, 1)

        @block.scalar
        def _(act):
            def exponentials(r, e, u):
                g = 2 * r + e
                n = g * SU + u
                _, _, q0 = S_UNITS[u]
                act.wait_ge(pv_done, n + 1)
                for pair in range(2):
                    act.wait_ge(s_done, 2 * n + pair + 1)
                    act.activation(probs[u % 2][:, 2 * pair:2 * pair + 2, q0:], s_ps[pair][:, :, q0:], ACT.Exp,
                                   scale=SCALE).then_inc(exp_done, 1)

            def take_shift(r, e, qc):
                g = 2 * r + e
                act.wait_ge(t_done, QC * g + qc + 1)
                act.wait_ge(shift_loaded[qc], 16 * QPK * g)
                act.activation(shift_t[qc][:], t_ps[:], ACT.Copy).then_inc(shift_t_ready, 1)

            def take_sums(r, e, qc):
                g = 2 * r + e
                act.wait_ge(pv_done, g * SU + CHUNK_LAST[qc] + 1 + 2)
                act.activation(heads_out[:, bass.ds(g * T + qc * N, N)], o_ps[:], ACT.Copy).then_inc(o_taken, 1)

            def group(r, e, last=False):
                r1, e1 = after(r, e)
                for u in range(SU):
                    if u < SU - 1:
                        exponentials(r, e, u + 1)
                    elif not last:
                        exponentials(r1, e1, 0)
                    if u == SHIFT_SECOND:
                        take_shift(r, e, 1)
                    if u == SHIFT_FIRST and not last:
                        take_shift(r1, e1, 0)
                    if u in CHUNK_LAST:
                        take_sums(r, e, CHUNK_LAST.index(u))

            take_shift(0, 0, 0)
            exponentials(0, 0, 0)
            with act.Fori(0, ROUNDS - 1) as r:
                group(r, 0)
                group(r, 1)
            group(ROUNDS - 1, 0)
            group(ROUNDS - 1, 1, last=True)

        @block.gpsimd
        def _(pool):
            def mask(r, e, u):
                g = 2 * r + e
                _, _, q0 = S_UNITS[u]
                wait_apart(pool, exp_done, 2 * (g * SU + u) + 2, passed)
                blk = probs[u % 2][:, :, q0:q0 + P]
                pool.affine_select(out=blk, in_=blk, compare_op=ALU.is_ge, fill=0.0, base=0,
                                   pattern=[[0, QPK], [1, P]], channel_multiplier=-1).then_inc(masked, 1)

            def stage_values(r, e):
                g = 2 * r + e
                pool.tensor_copy(vs[e][:, :, 0:HD], v.rearrange("p h (b k) d -> p (h b k) d", b=B)
                                 [:, bass.ds(g * KB, KB), :]).then_inc(v_staged, 1)

            def add_bias(r, e):
                tile = x[:, bass.ds(2 * r + e, 1), :].rearrange("p a c -> p (a c)")
                pool.tensor_tensor(tile, tile, bo[:], ALU.add).then_inc(x_biased, 1)

            def group(r, e, last=False):
                if not last:
                    pool.wait_ge(pv_done, (2 * r + e) * SU + 2)
                    stage_values(*after(r, e))
                for u in DIAGONAL:
                    mask(r, e, u)
                    if u == DIAGONAL[TPC - 1]:
                        add_bias(r, e)

            pool.memset(causal[:], 0.0).then_inc(masks_ready, 1)
            pool.wait_ge(masks_ready, 1)
            pool.affine_select(out=causal[:, N - P:], in_=causal[:, N - P:], compare_op=ALU.is_ge, fill=MASKED, base=0,
                               pattern=[[-1, P]], channel_multiplier=1).then_inc(masks_ready, 1)
            for e in range(2):
                pool.memset(sk[e][:], 1.0).then_inc(ones_ready, 1)
            for e in range(2):
                pool.memset(vs[e][:], 0.0).then_inc(ones_ready, 1)
            pool.wait_ge(ones_ready, 4)
            for e in range(2):
                pool.memset(vs[e][:, :, HD:HD + 1], 1.0).then_inc(ones_ready, 1)
            pool.wait_ge(ones_ready, 6)
            stage_values(0, 0)
            pool.wait_ge(bo_loaded, 16)
            with pool.Fori(0, ROUNDS - 1) as r:
                group(r, 0)
                group(r, 1)
            group(ROUNDS - 1, 0)
            group(ROUNDS - 1, 1, last=True)

        @block.sync
        def _(sp):
            q_groups = q_rows.rearrange("(g i j d) r t -> g j (d r) i t", i=QPK // 2, j=2, d=HD)
            k_groups = k_rows.rearrange("(g d) r t -> g (d r) t", d=HD)

            def load_m(r, e):
                tokens = slice(e * T, (e + 1) * T)
                for half in range(2):
                    rows = slice(HALF * half, HALF * half + ROWS)
                    sp.dma_start(mq[e][rows], q_groups[bass.ds(r, 1), half, :, :, tokens]
                                 .rearrange("g r i t -> r (g i) t")).then_inc(m_loaded[e], 16)
                    sp.dma_start(mk[e][rows], k_groups[bass.ds(r, 1), :, tokens]
                                 .rearrange("g r t -> r (g t)")).then_inc(m_loaded[e], 16)

            def copy_s(r, e):
                sp.wait_ge(m_loaded[e], 16 * 4 * (r + 1))
                for half in range(2):
                    rows = slice(HALF * half, HALF * half + ROWS)
                    sp.dma_start(sq[e][rows], mq[e][rows]).then_inc(s_loaded[e], 16)
                    sp.dma_start(sk[e][rows], mk[e][rows]).then_inc(s_loaded[e], 16)

            def load_shift(r, e, qc):
                sp.wait_ge(shift_t_ready, QC * (2 * r + e) + qc + 1)
                for h in range(QPK):
                    row = HALF * (h % 2) + ROWS
                    sp.dma_start(sq[e][row:row + SHIFT, h // 2, qc * N:(qc + 1) * N],
                                 shift_t[qc][h * SHIFT:(h + 1) * SHIFT, :]).then_inc(shift_loaded[qc], 16)

            def group(r, e, loads=True, last=False):
                g = 2 * r + e
                r1, e1 = after(r, e)
                load_shift(r, e, 1)
                if not last:
                    sp.wait_ge(s_done, 2 * SU * g)
                    copy_s(r1, e1)
                if loads:
                    sp.wait_ge(s_loaded[e], 16 * 4 * (r + 1))
                    sp.wait_ge(m_done, MU * (g + 1))
                    load_m(r + 1, e)
                if not last:
                    load_shift(r1, e1, 0)

            sp.dma_start(bo[:], bo_row.partition_broadcast(P)).then_inc(bo_loaded, 16)
            load_m(0, 0)
            load_m(0, 1)
            sp.wait_ge(ones_ready, 2)
            copy_s(0, 0)
            load_shift(0, 0, 0)
            with sp.Fori(0, ROUNDS - 1) as r:
                group(r, 0)
                group(r, 1)
            group(ROUNDS - 1, 0, loads=False)
            group(ROUNDS - 1, 1, loads=False, last=True)
            sp.wait_ge(o_taken, QC * GROUPS)
            sp.wait_ge(x_biased, GROUPS)


def output_phase(nc, heads_out, wo, ident, x, KVH, HD):
    _, TILES, C = x.shape
    KT = C // P
    HPK = C // HD // KVH
    tiles = heads_out.rearrange("p (h n) -> p h n", h=KVH)
    with ExitStack() as ctx:
        def sb(name, shape, dt):
            return [ctx.enter_context(nc.sbuf_tensor(f"out_{name}{e}", shape, dt)) for e in range(2)]

        def pb(name, shape):
            return [ctx.enter_context(nc.psum_tensor(f"out_{name}{e}", shape, F32)) for e in range(2)]

        def sem(name):
            return ctx.enter_context(nc.semaphore(f"out_{name}"))

        sums = sb("sums", [P, KVH, P], F32)
        inverse = sb("inverse", [P, KVH * HPK, 1], F32)
        attn = sb("attn", [P, KVH * HPK, HD], F32)
        at_hi = sb("at_hi", [P, KT, P], F32R)
        at_lo = sb("at_lo", [P, KT, P], F32R)
        sums_ps = pb("sums_ps", [P, KVH, P])
        at_ps = pb("at_ps", [P, KT, P])
        y_ps = pb("y_ps", [P, C])

        staged = sem("staged")
        sums_done = sem("sums_done")
        inverse_ready = sem("inverse_ready")
        attn_ready = sem("attn_ready")
        at_done = sem("at_done")
        hi_ready = sem("hi_ready")
        lo_ready = sem("lo_ready")
        y_done = sem("y_done")
        y_added = sem("y_added")
        block = ctx.enter_context(nc.Block())
        ROUNDS = TILES // 2

        def skewed(engine, steps):
            S = len(steps) - 1
            FIRST = (S + 3) // 2

            def tile(n, e, low=0, high=len(steps)):
                for k in range(low, high):
                    steps[k](n - k, (e - k) % 2)

            for n in range(2 * FIRST):
                tile(n, n % 2, high=min(n, S) + 1)
            with engine.Fori(FIRST, ROUNDS) as r:
                tile(2 * r, 0)
                tile(2 * r + 1, 1)
            for n in range(TILES, TILES + S):
                tile(n, n % 2, low=n - TILES + 1)

        def before(engine, signal, n):
            if not (isinstance(n, int) and n < 2):
                engine.wait_ge(signal, n - 1)

        @block.gpsimd
        def _(pool):
            def stage(n, e):
                before(pool, sums_done, n)
                pool.tensor_copy(sums[e][:], tiles[:, :, bass.ds(n * P, P)]).then_inc(staged, 1)

            skewed(pool, [stage])

        @block.tensor
        def _(pe):
            def transpose_sums(n, e):
                pe.wait_ge(staged, n + 1)
                before(pe, attn_ready, n)
                for h in range(KVH):
                    last = pe.transpose(sums_ps[e][:, h, :], sums[e][:, h, :], ident[:])
                last.then_inc(sums_done, 1)

            def transpose_attn(n, e):
                pe.wait_ge(attn_ready, n + 1)
                before(pe, lo_ready, n)
                flat = attn[e][:].rearrange("p h d -> p (h d)")
                for k in range(KT):
                    last = pe.transpose(at_ps[e][:, k, :], flat[:, k * P:(k + 1) * P], ident[:])
                last.then_inc(at_done, 1)

            def project(n, e):
                pe.wait_ge(hi_ready, n + 1)
                pe.wait_ge(lo_ready, n + 1)
                before(pe, y_added, n)
                i = 0
                for k in range(KT):
                    for hs, ws in ((at_hi[e], wo[0]), (at_hi[e], wo[1]), (at_lo[e], wo[0])):
                        last = pe.matmul(y_ps[e][:], hs[:, k, :], ws[:, k, :], start=(i == 0), stop=(i == 3 * KT - 1))
                        i += 1
                last.then_inc(y_done, 1)

            skewed(pe, [transpose_sums, transpose_attn, project])

        @block.scalar
        def _(act):
            def high_part(n, e):
                act.wait_ge(at_done, n + 1)
                before(act, y_done, n)
                act.activation(at_hi[e][:], at_ps[e][:], ACT.Copy).then_inc(hi_ready, 1)

            skewed(act, [high_part])

        @block.vector
        def _(dve):
            def divide(n, e):
                dve.wait_ge(sums_done, n + 1)
                before(dve, at_done, n)
                rows = sums_ps[e][:].rearrange("p g (j d) -> p (g j) d", j=HPK)
                dve.reciprocal(inverse[e][:], rows[:, :, HD:HD + 1]).then_inc(inverse_ready, 1)
                dve.wait_ge(inverse_ready, n + 1)
                dve.tensor_tensor(attn[e][:], rows[:, :, 0:HD], inverse[e][:].to_broadcast([P, KVH * HPK, HD]),
                                  ALU.mult).then_inc(attn_ready, 1)

            def low_part(n, e):
                dve.wait_ge(hi_ready, n + 1)
                dve.tensor_tensor(at_lo[e][:], at_ps[e][:], at_hi[e][:].bitcast(F32), ALU.subtract).then_inc(lo_ready, 1)

            def add(n, e):
                dve.wait_ge(y_done, n + 1)
                tile = x[:, bass.ds(n, 1), :].rearrange("p a c -> p (a c)")
                dve.tensor_tensor(tile, y_ps[e][:], tile, ALU.add).then_inc(y_added, 1)

            skewed(dve, [divide, low_part, add])

        @block.sync
        def _(sp):
            sp.wait_ge(y_added, TILES)


def load_phase(nc, x, x_rows, ident, ident_bf, splits, x_loaded, ident_ready, weights_ready):
    with ExitStack() as ctx:
        raws = [ctx.enter_context(nc.sbuf_tensor(f"raw{n}", shape, F32)) for n, (_, shape, _) in enumerate(splits)]
        loaded = [ctx.enter_context(nc.semaphore(f"raw_loaded{n}")) for n in range(len(splits))]
        hi_done = ctx.enter_context(nc.semaphore("w_hi_done"))
        lo_done = ctx.enter_context(nc.semaphore("w_lo_done"))
        block = ctx.enter_context(nc.Block())
        pieces = [(n, read(raw), hi, lo) for n, (raw, (_, _, ps)) in enumerate(zip(raws, splits)) for read, hi, lo in ps]

        @block.sync
        def _(sp):
            sp.dma_start(x[:], x_rows).then_inc(x_loaded, 16)
            for raw, (rows, _, _), sem in zip(raws, splits, loaded):
                sp.dma_start(raw[:], rows).then_inc(sem, 16)

        @block.gpsimd
        def _(pool):
            make_identity(pool, ident, ident_ready)
            pool.wait_ge(ident_ready, 2)
            pool.tensor_copy(ident_bf[:], ident[:]).then_inc(ident_ready, 1)

        @block.scalar
        def _(act):
            for n, src, hi, _ in pieces:
                act.wait_ge(loaded[n], 16)
                act.activation(hi, src, ACT.Copy).then_inc(hi_done, 1)

        @block.vector
        def _(dve):
            for i, (n, src, hi, lo) in enumerate(pieces):
                dve.wait_ge(hi_done, i + 1)
                dve.tensor_tensor(lo, src, hi.bitcast(F32), ALU.subtract).then_inc(lo_done, 1)
            dve.wait_ge(lo_done, len(pieces))
            dve.wait_ge(ident_ready, 3)
            dve.sem_inc(weights_ready, 1)


def build(nc, x_in, w_qkv, bias_cols, bv, w_o, bo, w_gate, w_up, w_down, cos_t, sin_t, out, HD=8, SPLIT=6):
    B, T, C = x_in.shape
    TILES = B * T // P
    HID = w_gate.shape[1]
    KT, BLKS, J = C // P, HID // 512, 4
    KV = bv.shape[0]
    KVH = KV // HD
    with ExitStack() as ctx:
        def sb(name, shape, dt, on=ctx):
            return on.enter_context(nc.sbuf_tensor(name, shape, dt))

        def sem(name):
            return ctx.enter_context(nc.semaphore(name))

        x = sb("x", [P, TILES, C], F32)
        ident = sb("ident", [P, P], F32)
        ident_bf = sb("ident_bf", [P, P], BF16)
        parts = ("hi", "lo")
        wg = [sb(f"wg_{n}", [P, KT, BLKS, J, P], F32R) for n in parts]
        wu = [sb(f"wu_{n}", [P, KT, BLKS, J, P], F32R) for n in parts]
        wd = [sb(f"wd_{n}", [P, BLKS, J, C], F32R) for n in parts]
        wqkv = [sb(f"wqkv_{n}", [P, KT, w_qkv.shape[1]], F32R) for n in parts]
        wo = [sb(f"wo_{n}", [P, KT, C], F32R) for n in parts]
        x_loaded, ident_ready, weights_ready = sem("x_loaded"), sem("ident_ready"), sem("weights_ready")
        x_rows = x_in.rearrange("b (t p) c -> p (b t) c", p=P)
        out_rows = out.rearrange("b (t p) c -> p (b t) c", p=P)
        q_rows = nc.dram_tensor("q_rows", [C, SPLIT, B * T], BF16).ap()
        k_rows = nc.dram_tensor("k_rows", [KV, SPLIT, B * T], BF16).ap()

        def by_blocks(w):
            return [(lambda raw, k=k, b=b: raw[:, k, b * 512:(b + 1) * 512].rearrange("q (p j) -> q j p", j=J),
                     w[0][:, k, b], w[1][:, k, b]) for b in range(BLKS) for k in range(KT)]

        def whole(w):
            return [(lambda raw: raw[:], w[0][:], w[1][:])]

        splits = [(w_gate.rearrange("(k p) n -> p k n", p=P), [P, KT, HID], by_blocks(wg)),
                  (w_up.rearrange("(k p) n -> p k n", p=P), [P, KT, HID], by_blocks(wu)),
                  (w_down.rearrange("(b p j) c -> p b j c", p=P, j=J), [P, BLKS, J, C], whole(wd)),
                  (w_qkv.rearrange("(k p) n -> p k n", p=P), [P, KT, w_qkv.shape[1]], whole(wqkv)),
                  (w_o.rearrange("(k p) n -> p k n", p=P), [P, KT, C], whole(wo))]
        load_phase(nc, x, x_rows, ident, ident_bf, splits, x_loaded, ident_ready, weights_ready)
        ffn_phase(nc, "ffn1", x, (wg, wu, wd), ident, weights_ready, x_loaded, None)
        with ExitStack() as attention:
            v = sb("v", [P, KVH, TILES, HD], F32, attention)
            qkv_phase(nc, x, ident, wqkv, bias_cols, bv, cos_t, sin_t, q_rows, k_rows, v)
            heads_out = sb("heads_out", [P, KVH * B * T], F32, attention)
            attention_phase(nc, q_rows, k_rows, v, heads_out, ident_bf, x, bo, T, HD)
            output_phase(nc, heads_out, wo, ident, x, KVH, HD)
        ffn_phase(nc, "ffn2", x, (wg, wu, wd), ident, weights_ready, x_loaded, out_rows)


def rope_tables(T, B, HD):
    import numpy as np

    inverse = (1.0 / np.float32(ROPE_BASE) ** (np.arange(0, HD, 2, dtype=np.float32) / np.float32(HD))).astype(np.float32)
    angles = np.outer(np.arange(T, dtype=np.float32), inverse).astype(np.float32)
    cos = np.repeat(np.cos(angles), 2, axis=1).T
    sin = np.repeat(np.sin(angles), 2, axis=1).T * np.tile(np.array([[-1.0], [1.0]], np.float32), (HD // 2, 1))
    return (np.ascontiguousarray(np.tile(cos, (P // HD, B)), dtype=np.float32),
            np.ascontiguousarray(np.tile(sin, (P // HD, B)), dtype=np.float32))


def swapped(a):
    return a.reshape(*a.shape[:-1], -1, 2)[..., ::-1].reshape(a.shape)


def kernel(**inputs):
    import numpy as np
    import concourse.bacc as bacc
    from concourse.bass_utils import run_bass_kernel_spmd

    a = {name.split("_", 1)[1]: np.asarray(value) for name, value in inputs.items()}
    x = a["attn_x"]
    B, T, C = x.shape
    HD = 8
    wq, wk, bq, bk = a["attn_Wq"], a["attn_Wk"], a["attn_bq"], a["attn_bk"]
    tiles = [wq[:, :P], wq[:, P:], np.concatenate([wk, wk], axis=1)]
    w_qkv = np.concatenate([w for t in tiles for w in (t, swapped(t))] + [a["attn_Wv"]], axis=1)
    b_tiles = [bq[:P], bq[P:], np.concatenate([bk, bk])]
    bias_cols = np.stack([b for t in b_tiles for b in (t, swapped(t))], axis=1)
    cos_t, sin_t = rope_tables(T, B, HD)
    arrays = {"x": x, "w_qkv": w_qkv, "bias_cols": bias_cols, "bv": a["attn_bv"], "w_o": a["attn_Wo"], "bo": a["attn_bo"],
              "w_gate": a["ffn_w_gate"], "w_up": a["ffn_w_up"], "w_down": a["ffn_w_down"], "cos_t": cos_t, "sin_t": sin_t}
    nc = bacc.Bacc("TRN2", target_bir_lowering=False, num_devices=1)
    arrays = {f"in_{name}": np.ascontiguousarray(value) for name, value in arrays.items()}
    args = [nc.dram_tensor(name, value.shape, mybir.dt.from_np(value.dtype), kind="ExternalInput").ap()
            for name, value in arrays.items()]
    out = nc.dram_tensor("out", x.shape, F32, kind="ExternalOutput").ap()
    build(nc, *args, out)
    result = run_bass_kernel_spmd(nc, [arrays], core_ids=[0])
    return result.results[0]["out"]
```

```python
import concourse.bass as bass
from concourse import mybir
from contextlib import ExitStack

F32 = mybir.dt.float32
F32R = mybir.dt.float32r
BF16 = mybir.dt.bfloat16
ALU = mybir.AluOpType
ACT = mybir.ActivationFunctionType

P = 128
EPS = 1e-5
ROPE_BASE = 10000.0
MASKED = -1.0e30


class Steps:

    def __init__(self, sem, per_round):
        self.sem, self.per_round, self.n = sem, per_round, 0

    def mark(self, instruction):
        self.n += 1
        return instruction.then_inc(self.sem, 1)

    def value(self, round_index):
        return self.n + self.per_round * round_index


def wait_apart(engine, sem, value, passed):
    engine.wait_ge(sem, value)
    engine.sem_inc(passed, 1)


def make_identity(pool, ident, signal):
    pool.memset(ident[:], 0.0).then_inc(signal, 1)
    pool.wait_ge(signal, 1)
    pool.affine_select(out=ident[:], in_=ident[:], compare_op=ALU.not_equal, fill=1.0, base=0,
                       pattern=[[-1, P]], channel_multiplier=1).then_inc(signal, 1)


class NormedChunks:

    def __init__(self, nc, ctx, tag, x, ident, N):
        _, self.TILES, self.C = x.shape
        self.x, self.ident, self.N = x, ident, N
        self.TPC = N // P
        self.KT = self.C // P
        TPC, C, KT = self.TPC, self.C, self.KT

        def sb(name, shape, dt):
            return ctx.enter_context(nc.sbuf_tensor(f"{tag}_{name}", shape, dt))

        def sem(name):
            return ctx.enter_context(nc.semaphore(f"{tag}_{name}"))

        self.stats = sb("stats", [P, TPC, 6], F32)
        self.mean_var = sb("mean_var", [P, TPC, 2], F32)
        self.var_eps = sb("var_eps", [P, TPC], F32)
        self.rstd = sb("rstd", [P, TPC], F32)
        self.minus_half = sb("minus_half", [P, TPC], F32)
        self.xn = sb("xn", [P, TPC, C], F32)
        self.xt_hi = sb("xt_hi", [P, KT, N], F32R)
        self.xt_lo = sb("xt_lo", [P, KT, N], F32R)
        self.xt_ps = ctx.enter_context(nc.psum_tensor(f"{tag}_xt_ps", [P, KT, N], F32))
        self.passed = sem("passed")
        self.stats_step = sem("stats_step")
        self.stats_ready = sem("stats_ready")
        self.var_ready = sem("var_ready")
        self.rstd_ready = sem("rstd_ready")
        self.xn_ready = sem("xn_ready")
        self.xt_done = sem("xt_done")
        self.hi_ready = sem("xt_hi_ready")
        self.lo_ready = sem("xt_lo_ready")

    def x_tile(self, c, t):
        return self.x[:, bass.ds(c * self.TPC + t, 1), :].rearrange("p a c -> p (a c)")

    def statistics(self, dve, c):
        for t in range(self.TPC):
            dve.bn_stats(self.stats[:, t, :], self.x_tile(c, t)).then_inc(self.stats_step, 1)
        for t in range(self.TPC):
            wait_apart(dve, self.stats_step, c * self.TPC + t + 1, self.passed)
            last = dve.bn_aggr(self.mean_var[:, t, :], self.stats[:, t, :])
        last.then_inc(self.stats_ready, 1)

    def exponents(self, pool):
        pool.memset(self.minus_half[:], -0.5).then_inc(self.var_ready, 1)

    def inverse_deviation(self, pool, c):
        wait_apart(pool, self.stats_ready, c + 1, self.passed)
        pool.tensor_scalar(self.var_eps[:], self.mean_var[:, :, 1], EPS, None, ALU.add).then_inc(self.var_ready, 1)
        pool.wait_ge(self.var_ready, c + 2)
        pool.tensor_tensor(self.rstd[:], self.var_eps[:], self.minus_half[:], ALU.pow).then_inc(self.rstd_ready, 1)

    def normalise(self, dve, c):
        dve.wait_ge(self.rstd_ready, c + 1)
        for t in range(self.TPC):
            last = dve.tensor_scalar(self.xn[:, t, :], self.x_tile(c, t), self.mean_var[:, t, 0:1],
                                     self.rstd[:, t:t + 1], ALU.subtract, ALU.mult)
        last.then_inc(self.xn_ready, 1)

    def transpose(self, pe, c):
        pe.wait_ge(self.xn_ready, c + 1)
        for t in range(self.TPC):
            for k in range(self.KT):
                last = pe.transpose(self.xt_ps[:, k, t * P:(t + 1) * P], self.xn[:, t, k * P:(k + 1) * P],
                                    self.ident[:])
        last.then_inc(self.xt_done, 1)

    def high_parts(self, act, c):
        act.wait_ge(self.xt_done, c + 1)
        act.activation(self.xt_hi[:], self.xt_ps[:], ACT.Copy).then_inc(self.hi_ready, 1)

    def low_parts(self, dve, c):
        dve.wait_ge(self.hi_ready, c + 1)
        dve.tensor_tensor(self.xt_lo[:], self.xt_ps[:], self.xt_hi[:].bitcast(F32), ALU.subtract)\
           .then_inc(self.lo_ready, 1)

    def wait_split(self, pe, c):
        pe.wait_ge(self.hi_ready, c + 1)
        pe.wait_ge(self.lo_ready, c + 1)


def ffn_phase(nc, tag, x, weights, ident, weights_ready, x_ready, out_rows):
    _, TILES, C = x.shape
    KT = C // P
    wg, wu, wd = weights
    BLKS = wd[0].shape[1]
    J = 4
    N = 512
    TPC = N // P
    CHUNKS = TILES // TPC
    assert BLKS == 2 and CHUNKS >= 3

    with ExitStack() as ctx:
        def sb(name, shape, dt):
            return ctx.enter_context(nc.sbuf_tensor(f"{tag}_{name}", shape, dt))

        def pb(name, shape, dt=F32):
            return ctx.enter_context(nc.psum_tensor(f"{tag}_{name}", shape, dt))

        def sem(name):
            return ctx.enter_context(nc.semaphore(f"{tag}_{name}"))

        normed = NormedChunks(nc, ctx, tag, x, ident, N)
        silu = sb("silu", [P, 2, N], F32)
        h = sb("h", [P, J, N], F32)
        a = sb("a", [P, J, N], F32)
        pair_max = sb("pair_max", [P, 2, N], F32)
        pair_min = sb("pair_min", [P, 2, N], F32)
        first_wins = sb("first_wins", [P, 2, N], BF16)
        both_low = sb("both_low", [P, N], BF16)
        both_high = sb("both_high", [P, N], BF16)
        tilt = sb("tilt", [P, N], BF16)
        rank = sb("rank", [P, J, N], BF16)
        hs = sb("hs", [P, J, N], F32)
        hs_hi = sb("hs_hi", [P, BLKS, J, N], F32R)
        hs_lo = sb("hs_lo", [P, BLKS, J, N], F32R)

        gu = [[pb(f"{w}{i}", [P, N]) for w in ("gate", "up")] for i in range(2)]
        y_ps = pb("y_ps", [P, TPC, C])

        gu_done = sem("gu_done")
        silu_ready = sem("silu_ready")
        h_ready = sem("h_ready")
        abs_ready = sem("abs_ready")
        dve_step = sem("dve_step")
        hs_ready = sem("hs_ready")
        hi_ready = sem("hi_ready")
        lo_ready = sem("lo_ready")
        hs_free = sem("hs_free")
        y_done = sem("y_done")
        y_added = sem("y_added")
        stored = sem("stored")

        block = ctx.enter_context(nc.Block())

        @block.tensor
        def _(pe):
            def gate_up(c, blk, first=False):
                if blk == 0:
                    normed.wait_split(pe, c)
                for j in range(J):
                    i = j % 2
                    if not (first and j < 2):
                        pe.wait_ge(h_ready, (c * BLKS + blk) * J + j - 1)
                    for w, ps in zip((wg, wu), gu[i]):
                        n = 0
                        for k in range(KT):
                            for ws, xs in ((w[0], normed.xt_hi), (w[1], normed.xt_hi), (w[0], normed.xt_lo)):
                                last = pe.matmul(ps[:], ws[:, k, blk, j, :], xs[:, k, :],
                                                 start=(n == 0), stop=(n == 3 * KT - 1))
                                n += 1
                    last.then_inc(gu_done, 1)

            def down(c, blk):
                if blk == 0:
                    pe.wait_ge(y_added, c)
                for j in range(J):
                    n = (c * BLKS + blk) * J + j + 1
                    pe.wait_ge(hi_ready, n)
                    pe.wait_ge(lo_ready, n)
                    for t in range(TPC):
                        rows = slice(t * P, (t + 1) * P)
                        for m, (hp, wp) in enumerate(((hs_hi, wd[0]), (hs_hi, wd[1]), (hs_lo, wd[0]))):
                            last = pe.matmul(y_ps[:, t, :], hp[:, blk, j, rows], wp[:, blk, j, :],
                                             start=(blk == 0 and j == 0 and m == 0 and t % 2 == 0),
                                             stop=(blk == BLKS - 1 and j == J - 1 and m == 2),
                                             skip_group_check=True)
                last.then_inc(hs_free, 1)
                if blk == BLKS - 1:
                    pe.drain().then_inc(y_done, 1)

            pe.sem_inc(hs_free, BLKS)
            pe.wait_ge(weights_ready, 1)
            normed.transpose(pe, 0)
            gate_up(0, 0, first=True)
            with pe.Fori(0, CHUNKS - 1) as c:
                gate_up(c, 1)
                normed.transpose(pe, c + 1)
                down(c, 0)
                gate_up(c + 1, 0)
                down(c, 1)
            gate_up(CHUNKS - 1, 1)
            down(CHUNKS - 1, 0)
            down(CHUNKS - 1, 1)

        @block.scalar
        def _(act):
            def silu_of(c, blk, j):
                n = (c * BLKS + blk) * J + j
                act.wait_ge(gu_done, n + 1)
                act.activation(silu[:, j % 2, :], gu[j % 2][0][:], ACT.Silu).then_inc(silu_ready, 1)

            def abs_of(c, blk, j):
                act.wait_ge(h_ready, (c * BLKS + blk) * J + j + 1)
                act.activation(a[:, j, :], h[:, j, :], ACT.Abs).then_inc(abs_ready, 1)

            def hidden(c, blk):
                for j in range(J):
                    silu_of(c, blk, j)
                    if j:
                        abs_of(c, blk, j - 1)
                abs_of(c, blk, J - 1)

            def high_parts(c, blk):
                act.wait_ge(hs_free, c * BLKS + blk + 1)
                for j in range(J):
                    act.wait_ge(hs_ready, (c * BLKS + blk) * J + j + 1)
                    act.activation(hs_hi[:, blk, j, :], hs[:, j, :], ACT.Copy).then_inc(hi_ready, 1)

            normed.high_parts(act, 0)
            with act.Fori(0, CHUNKS - 1) as c:
                hidden(c, 0)
                high_parts(c, 0)
                hidden(c, 1)
                normed.high_parts(act, c + 1)
                high_parts(c, 1)
            hidden(CHUNKS - 1, 0)
            high_parts(CHUNKS - 1, 0)
            hidden(CHUNKS - 1, 1)
            high_parts(CHUNKS - 1, 1)

        @block.vector
        def _(dve):
            step = Steps(dve_step, per_round=BLKS * 10)

            def hidden(c, blk):
                for j in range(J):
                    dve.wait_ge(silu_ready, (c * BLKS + blk) * J + j + 1)
                    dve.tensor_tensor(h[:, j, :], gu[j % 2][1][:], silu[:, j % 2, :], ALU.mult).then_inc(h_ready, 1)

            def sparsify(c, blk):
                dve.wait_ge(abs_ready, (c * BLKS + blk + 1) * J)
                step.mark(dve.tensor_tensor(pair_max[:], a[:, 0::2, :], a[:, 1::2, :], ALU.max))
                step.mark(dve.tensor_tensor(pair_min[:], a[:, 0::2, :], a[:, 1::2, :], ALU.min))
                step.mark(dve.tensor_tensor(first_wins[:], a[:, 0::2, :], a[:, 1::2, :], ALU.is_ge))
                dve.wait_ge(dve_step, step.value(c) - 1)
                step.mark(dve.tensor_tensor(both_low[:], pair_min[:, 0, :], pair_max[:, 1, :], ALU.is_ge))
                step.mark(dve.tensor_tensor(both_high[:], pair_min[:, 1, :], pair_max[:, 0, :], ALU.is_gt))
                dve.wait_ge(dve_step, step.value(c))
                step.mark(dve.tensor_tensor(tilt[:], both_low[:], both_high[:], ALU.subtract))
                dve.wait_ge(dve_step, step.value(c))
                for j, op in enumerate((ALU.add, ALU.subtract, ALU.subtract, ALU.add)):
                    step.mark(dve.tensor_tensor(rank[:, j, :], first_wins[:, j // 2, :], tilt[:], op))
                at = step.value(c)
                dve.wait_ge(hi_ready, (c * BLKS + blk) * J)
                dve.wait_ge(lo_ready, (c * BLKS + blk) * J)
                for j, (op, bound) in enumerate(((ALU.is_ge, 1.0), (ALU.is_le, 0.0), (ALU.is_ge, 1.0), (ALU.is_le, 0.0))):
                    dve.wait_ge(dve_step, at - 3 + j)
                    dve.scalar_tensor_tensor(out=hs[:, j, :], in0=rank[:, j, :], scalar=bound, in1=h[:, j, :],
                                             op0=op, op1=ALU.mult).then_inc(hs_ready, 1)

            def add_down(c):
                dve.wait_ge(y_done, c + 1)
                rows = x[:, bass.ds(c * TPC, TPC), :].rearrange("p t c -> p (t c)")
                dve.scalar_tensor_tensor(out=rows, in0=y_ps[:].rearrange("p t c -> p (t c)"), scalar=0.5, in1=rows,
                                         op0=ALU.mult, op1=ALU.add).then_inc(y_added, 1)

            def chunk(c, first=False, last=False):
                step.n = 0
                if not last:
                    normed.statistics(dve, c + 1)
                hidden(c, 0)
                sparsify(c, 0)
                if not first:
                    add_down(c - 1)
                if not last:
                    normed.normalise(dve, c + 1)
                hidden(c, 1)
                if not last:
                    normed.low_parts(dve, c + 1)
                sparsify(c, 1)
                assert last or step.n == step.per_round

            dve.wait_ge(x_ready, 16)
            normed.statistics(dve, 0)
            normed.normalise(dve, 0)
            normed.low_parts(dve, 0)
            chunk(0, first=True)
            with dve.Fori(1, CHUNKS - 1) as c:
                chunk(c)
            chunk(CHUNKS - 1, last=True)
            add_down(CHUNKS - 1)

        @block.gpsimd
        def _(pool):
            def low_parts(c, blk):
                pool.wait_ge(hs_free, c * BLKS + blk + 1)
                for j in range(J):
                    pool.wait_ge(hi_ready, (c * BLKS + blk) * J + j + 1)
                    pool.tensor_tensor(hs_lo[:, blk, j, :], hs[:, j, :], hs_hi[:, blk, j, :].bitcast(F32),
                                       ALU.subtract).then_inc(lo_ready, 1)

            normed.exponents(pool)
            normed.inverse_deviation(pool, 0)
            with pool.Fori(0, CHUNKS - 1) as c:
                normed.inverse_deviation(pool, c + 1)
                low_parts(c, 0)
                low_parts(c, 1)
            low_parts(CHUNKS - 1, 0)
            low_parts(CHUNKS - 1, 1)

        @block.sync
        def _(sp):
            if out_rows is not None:
                with sp.Fori(0, CHUNKS) as c:
                    sp.wait_ge(y_added, c + 1)
                    sp.dma_start(out_rows[:, bass.ds(c * TPC, TPC), :],
                                 x[:, bass.ds(c * TPC, TPC), :]).then_inc(stored, 16)
                sp.wait_ge(stored, CHUNKS * 16)
            else:
                sp.wait_ge(y_added, CHUNKS)


def qkv_phase(nc, x, ident, wqkv, bias_cols, bv_row, cos_t, sin_t, q_rows, k_rows, v):
    w_hi, w_lo = wqkv
    N = 512
    B_T = x.shape[1] * P
    CHUNKS = B_T // N
    QM = 2
    UNITS = QM + 1
    _, KVH, _, HD = v.shape
    KV = KVH * HD

    with ExitStack() as ctx:
        def sb(name, shape, dt):
            return ctx.enter_context(nc.sbuf_tensor(f"qkv_{name}", shape, dt))

        def pb(name, shape, dt=F32):
            return ctx.enter_context(nc.psum_tensor(f"qkv_{name}", shape, dt))

        def sem(name):
            return ctx.enter_context(nc.semaphore(f"qkv_{name}"))

        normed = NormedChunks(nc, ctx, "qkv", x, ident, N)
        TPC, KT = normed.TPC, normed.KT
        biases = sb("biases", [P, 2 * UNITS], F32)
        bv = sb("bv", [P, KV], F32)
        cos = sb("cos", [P, B_T], F32)
        sin = sb("sin", [P, B_T], F32)
        by_cos = sb("by_cos", [P, UNITS, N], F32)
        by_sin = sb("by_sin", [P, UNITS, N], F32)
        turned = sb("turned", [P, UNITS, N], F32)
        rest = sb("rest", [P, UNITS, N], F32)
        parts = sb("parts", [P, UNITS, 3, N], BF16)
        qk_ps = [[pb(f"{w}{i}", [P, N]) for w in ("plain", "swapped")] for i in range(2)]
        v_ps = pb("v_ps", [P, TPC, KV])

        tables_loaded = sem("tables_loaded")
        qk_done = sem("qk_done")
        v_done = sem("v_done")
        by_ready = sem("by_ready")
        turned_ready = sem("turned_ready")
        hi_ready = sem("hi_ready")
        rest_ready = sem("rest_ready")
        mid_ready = sem("mid_ready")
        lo_ready = sem("lo_ready")
        v_ready = sem("v_ready")
        stored = [sem(f"stored{u}") for u in range(UNITS)]
        PARTS = 3

        block = ctx.enter_context(nc.Block())

        @block.tensor
        def _(pe):
            def units(c, first=False):
                normed.wait_split(pe, c)
                for u in range(UNITS):
                    if not (first and u < 2):
                        pe.wait_ge(by_ready, c * UNITS + (0, -1, 1)[u])
                    for which in range(2):
                        col = (2 * u + which) * P
                        n = 0
                        for k in range(KT):
                            for ws, xs in ((w_hi, normed.xt_hi), (w_lo, normed.xt_hi), (w_hi, normed.xt_lo)):
                                last = pe.matmul(qk_ps[u % 2][which][:], ws[:, k, col:col + P], xs[:, k, :],
                                                 start=(n == 0), stop=(n == 3 * KT - 1))
                                n += 1
                    last.then_inc(qk_done, 1)

            def values(c):
                pe.wait_ge(v_ready, c)
                col = 2 * UNITS * P
                for t in range(TPC):
                    rows = slice(t * P, (t + 1) * P)
                    n = 0
                    for k in range(KT):
                        for ws, xs in ((w_hi, normed.xt_hi), (w_lo, normed.xt_hi), (w_hi, normed.xt_lo)):
                            last = pe.matmul(v_ps[:, t, :], xs[:, k, rows], ws[:, k, col:col + KV],
                                             start=(n == 0 and t == 0), stop=(n == 3 * KT - 1), skip_group_check=True)
                            n += 1
                last.then_inc(v_done, 1)

            normed.transpose(pe, 0)
            units(0, first=True)
            values(0)
            with pe.Fori(1, CHUNKS) as c:
                normed.transpose(pe, c)
                units(c)
                values(c)

        @block.scalar
        def _(act):
            def part(c, u, i):
                n = c * UNITS + u
                if i == 0:
                    act.wait_ge(turned_ready, n + 1)
                    act.wait_ge(stored[u], 16 * PARTS * c)
                    act.activation(parts[:, u, 0, :], turned[:, u, :], ACT.Copy).then_inc(hi_ready, 1)
                else:
                    act.wait_ge(rest_ready, n + 1)
                    act.activation(parts[:, u, 1, :], rest[:, u, :], ACT.Copy).then_inc(mid_ready, 1)

            with act.Fori(0, CHUNKS) as c:
                normed.high_parts(act, c)
                for u, i in ((0, 0), (1, 0), (0, 1), (2, 0), (1, 1), (2, 1)):
                    part(c, u, i)

        @block.vector
        def _(dve):
            def turn(c, u):
                n = c * UNITS + u
                dve.wait_ge(qk_done, n + 1)
                tokens = bass.ds(c * N, N)
                dve.scalar_tensor_tensor(out=by_cos[:, u, :], in0=qk_ps[u % 2][0][:], scalar=biases[:, 2 * u:2 * u + 1],
                                         in1=cos[:, tokens], op0=ALU.add, op1=ALU.mult)
                dve.scalar_tensor_tensor(out=by_sin[:, u, :], in0=qk_ps[u % 2][1][:],
                                         scalar=biases[:, 2 * u + 1:2 * u + 2], in1=sin[:, tokens],
                                         op0=ALU.add, op1=ALU.mult).then_inc(by_ready, 1)

            def lo_part(c, u):
                dve.wait_ge(mid_ready, c * UNITS + u + 1)
                dve.tensor_tensor(parts[:, u, 2, :], rest[:, u, :], parts[:, u, 1, :], ALU.subtract).then_inc(lo_ready, 1)

            def values(c):
                dve.wait_ge(v_done, c + 1)
                for h in range(KVH):
                    cols = slice(h * HD, (h + 1) * HD)
                    last = dve.tensor_tensor(v[:, h, bass.ds(c * TPC, TPC), :], v_ps[:, :, cols],
                                             bv[:, None, cols].to_broadcast([P, TPC, HD]), ALU.add)
                last.then_inc(v_ready, 1)

            def chunk(c, last=False):
                normed.low_parts(dve, c)
                turn(c, 0)
                turn(c, 1)
                lo_part(c, 0)
                if not last:
                    normed.statistics(dve, c + 1)
                turn(c, 2)
                lo_part(c, 1)
                if not last:
                    normed.normalise(dve, c + 1)
                values(c)
                lo_part(c, 2)

            normed.statistics(dve, 0)
            normed.normalise(dve, 0)
            dve.wait_ge(tables_loaded, 4 * 16)
            with dve.Fori(0, CHUNKS - 1) as c:
                chunk(c)
            chunk(CHUNKS - 1, last=True)

        @block.gpsimd
        def _(pool):
            def add_turned(c, u):
                pool.wait_ge(by_ready, c * UNITS + u + 1)
                pool.tensor_tensor(turned[:, u, :], by_cos[:, u, :], by_sin[:, u, :], ALU.add).then_inc(turned_ready, 1)

            def leave_rest(c, u):
                pool.wait_ge(hi_ready, c * UNITS + u + 1)
                pool.tensor_tensor(rest[:, u, :], turned[:, u, :], parts[:, u, 0, :], ALU.subtract).then_inc(rest_ready, 1)

            def chunk(c, last=False):
                add_turned(c, 0)
                add_turned(c, 1)
                leave_rest(c, 0)
                if not last:
                    normed.inverse_deviation(pool, c + 1)
                add_turned(c, 2)
                leave_rest(c, 1)
                leave_rest(c, 2)

            normed.exponents(pool)
            normed.inverse_deviation(pool, 0)
            with pool.Fori(0, CHUNKS - 1) as c:
                chunk(c)
            chunk(CHUNKS - 1, last=True)

        @block.sync
        def _(sp):
            sp.dma_start(biases[:], bias_cols).then_inc(tables_loaded, 16)
            sp.dma_start(bv[:], bv_row.partition_broadcast(P)).then_inc(tables_loaded, 16)
            sp.dma_start(cos[:], cos_t).then_inc(tables_loaded, 16)
            sp.dma_start(sin[:], sin_t).then_inc(tables_loaded, 16)
            with sp.Fori(0, CHUNKS) as c:
                tokens = bass.ds(c * N, N)
                for u in range(UNITS):
                    for part, ready in enumerate((hi_ready, mid_ready, lo_ready)):
                        rows = (q_rows[u * P:(u + 1) * P, PARTS * part:PARTS * (part + 1), tokens] if u < QM
                                else k_rows[:, part::PARTS, tokens])
                        src = parts[:rows.shape[0], u, part, :]
                        sp.wait_ge(ready, c * UNITS + u + 1)
                        sp.dma_start(rows, src[:, None, :].to_broadcast([rows.shape[0], PARTS, N]))\
                          .then_inc(stored[u], 16)
            for u in range(UNITS):
                sp.wait_ge(stored[u], 16 * PARTS * CHUNKS)
            sp.wait_ge(v_ready, CHUNKS)


def attention_phase(nc, q_rows, k_rows, v, sum_tiles, ident_bf, x, bo_row, T, HD):
    SPLIT = q_rows.shape[1]
    ROWS = SPLIT * HD
    SHIFT = 3
    HEADS = q_rows.shape[0] // HD
    KVH = k_rows.shape[0] // HD
    B = q_rows.shape[2] // T
    GROUPS = B * KVH
    QPK = HEADS // KVH
    KB = T // P
    N = 512
    QC = T // N
    TPC = N // P
    SCALE = 1.0 / float(HD) ** 0.5
    assert QPK == 4 and QC == 2 and GROUPS % 2 == 0 and ROWS + SHIFT <= P

    S_UNITS = [(qc, kb, max(0, kb * P - qc * N)) for qc in range(QC) for kb in range(TPC * (qc + 1))]
    SU = len(S_UNITS)
    DIAGONAL = [u for u, (qc, kb, _) in enumerate(S_UNITS) if kb >= TPC * qc]
    CHUNK_FIRST = [[q for q, _, _ in S_UNITS].index(qc) for qc in range(QC)]
    CHUNK_LAST = [first - 1 for first in CHUNK_FIRST[1:]] + [SU - 1]
    M_UNITS = [(t, h, kc, min(N, (t + 1) * P - kc * N)) for t in range(KB) for kc in range(t // TPC + 1)
               for h in range(QPK)]
    MU = len(M_UNITS)
    MU_HALF = TPC * QPK

    AHEAD = 2
    SHARES = (1 / 4, 1 / 4, 1 / 2)
    width = [N - q0 for _, _, q0 in S_UNITS]
    work = [width[u] + width[(u + AHEAD) % SU] for u in range(SU)]
    m_total = sum(n for *_, n in M_UNITS)
    M_AT = [[[] for _ in SHARES] for _ in range(SU)]
    done = upto = 0
    left_over = list(range(MU))
    order = [*range(SU - AHEAD, SU), *range(SU - AHEAD)]
    for u in order:
        for slot, share in enumerate(SHARES):
            upto += work[u] * share
            while left_over and done < m_total * upto / sum(work):
                m = left_over.pop(0)
                done += M_UNITS[m][3]
                M_AT[u][slot].append((1 + (u >= SU - AHEAD), m))
    M_AT[SU - AHEAD - 1][-1] += [(1, m) for m in left_over]
    SHIFT_AT = [next(u for u in order if any(m >= MU_HALF for slot in M_AT[u] for _, m in slot)) + 1, SU - AHEAD]
    assert 0 < SHIFT_AT[0] < SU - AHEAD
    M_BANKS = 3
    M_FIRST = sum(len(slot) for u in order[:AHEAD] for slot in M_AT[u])
    LENT = [M_FIRST + sum(len(slot) for units in M_AT[:SHIFT_AT[0]] for slot in units)
            + sum(map(len, M_AT[SHIFT_AT[0]][:2])), sum(map(len, M_AT[SHIFT_AT[1]][:2]))]
    LENT_START = [MU_HALF + QPK, M_FIRST - 1]
    assert MU % M_BANKS == 0 and SU % (AHEAD + 1) == 0 and MU_HALF < LENT[0] < MU

    with ExitStack() as ctx:
        def sb(name, shape, dt):
            return ctx.enter_context(nc.sbuf_tensor(f"att_{name}", shape, dt))

        def pb(name, shape, dt=F32):
            return ctx.enter_context(nc.psum_tensor(f"att_{name}", shape, dt))

        def sem(name):
            return ctx.enter_context(nc.semaphore(f"att_{name}"))

        mq = [sb(f"mq{e}", [P, QPK, T], BF16) for e in range(2)]
        mk = [sb(f"mk{e}", [P, T], BF16) for e in range(2)]
        sq = [sb(f"sq{e}", [P, QPK, T], BF16) for e in range(2)]
        sk = [sb(f"sk{e}", [P, T], BF16) for e in range(2)]
        vs = [sb(f"vs{e}", [P, KB, 32], F32) for e in range(2)]
        probs = [sb(f"probs{i}", [P, QPK, N], F32) for i in range(AHEAD + 1)]
        causal = sb("causal", [P, N], F32)
        scratch = [sb(f"scratch{i}", [P, N], BF16) for i in range(M_BANKS)]
        max_a = sb("max_a", [P, QPK, KB], F32)
        max_b = sb("max_b", [P, QPK, TPC], F32)
        max_ab = sb("max_ab", [P, TPC, QPK], F32)
        left = sb("left", [P, TPC, QPK], F32)
        shift = [sb(f"shift{i}", [P, TPC, QPK, SHIFT], BF16) for i in range(QC)]
        shift_t = [sb(f"shift_t{i}", [QPK * SHIFT, N], BF16) for i in range(QC)]
        sums = [sb(f"sums{qc}", [P, N], F32) for qc in range(QC)]
        bo = sb("bo", [P, x.shape[2]], F32)

        s_ps = [pb(f"s_ps{i}", [P, 2, N]) for i in range(2)]
        m_ps = [pb(f"m_ps{i}", [P, N]) for i in range(M_BANKS)]
        o_ps = pb("o_ps", [P, N])
        t_ps = [ps[:QPK * SHIFT, :N // 2].bitcast(BF16) for ps in m_ps]

        masks_ready = sem("masks_ready")
        ones_ready = sem("ones_ready")
        zeros_ready = sem("zeros_ready")
        m_loaded = [sem(f"m_loaded{e}") for e in range(2)]
        s_loaded = [sem(f"s_loaded{e}") for e in range(2)]
        shift_loaded = [sem(f"shift_loaded{i}") for i in range(QC)]
        bo_loaded = sem("bo_loaded")
        v_staged = sem("v_staged")
        m_done = sem("m_done")
        m_taken = sem("m_taken")
        max_step = sem("max_step")
        shift_ready = sem("shift_ready")
        t_done = sem("t_done")
        shift_t_ready = sem("shift_t_ready")
        s_done = sem("s_done")
        exp_done = sem("exp_done")
        masked = sem("masked")
        pv_done = sem("pv_done")
        o_taken = sem("o_taken")
        sums_stored = [sem(f"sums_stored{qc}") for qc in range(QC)]
        passed = sem("passed")
        x_biased = sem("x_biased")

        block = ctx.enter_context(nc.Block())

        def after(r, e):
            return (r, 1) if e == 0 else (r + 1, 0)

        ROUNDS = GROUPS // 2

        @block.tensor
        def _(pe):
            def m_unit(r, e, m, lent=None):
                g = 2 * r + e
                t, h, kc, n = M_UNITS[m]
                if lent is not None:
                    pe.wait_ge(shift_t_ready, lent + 1)
                if m == 0:
                    pe.wait_ge(m_loaded[e], 16 * 2 * (r + 1))
                if not (isinstance(g, int) and g * MU + m < M_BANKS):
                    pe.wait_ge(m_taken, g * MU + m - M_BANKS + 1)
                pe.matmul(m_ps[m % M_BANKS][:, :n], mq[e][:, h, t * P:(t + 1) * P], mk[e][:, kc * N:kc * N + n], start=True, stop=True).then_inc(m_done, 1)

            def transpose_shift(r, e, qc, g1, m):
                n = QC * (2 * r + e) + qc
                pe.wait_ge(shift_ready, n + 1)
                taken = g1 * MU + m - M_BANKS + 1
                pe.wait_ge(m_taken, min(taken, GROUPS * MU) if isinstance(g1, int) else taken)
                for t in range(TPC):
                    last = pe.transpose(t_ps[m % M_BANKS][:, t * P:(t + 1) * P],
                                        shift[qc][:, t, :, :].rearrange("p h s -> p (h s)"), ident_bf[:])
                last.then_inc(t_done, 1)
                return n

            def s_unit(r, e, u, pair):
                g = 2 * r + e
                n = g * SU + u
                qc, kb, q0 = S_UNITS[u]
                if pair == 0 and u == 0:
                    pe.wait_ge(s_loaded[e], 16 * 2 * (r + 1))
                if pair == 0 and u in CHUNK_FIRST:
                    pe.wait_ge(shift_loaded[qc], 16 * QPK * (g + 1))
                if not (isinstance(n, int) and n == 0):
                    pe.wait_ge(exp_done, 2 * n + pair - 1)
                for half in range(2):
                    last = pe.matmul(s_ps[pair][:, half, q0:], sk[e][:, kb * P:(kb + 1) * P],
                                     sq[e][:, 2 * pair + half, qc * N + q0:(qc + 1) * N], start=True, stop=True)
                last.then_inc(s_done, 1)

            def value_unit(r, e, u):
                g = 2 * r + e
                qc, kb, q0 = S_UNITS[u]
                n = g * SU + u
                if u == 0:
                    pe.wait_ge(v_staged, g + 1)
                if u in CHUNK_FIRST:
                    pe.wait_ge(o_taken, QC * g + qc)
                pe.wait_ge(exp_done, 2 * n + 2)
                if u in DIAGONAL:
                    pe.wait_ge(masked, g * len(DIAGONAL) + DIAGONAL.index(u) + 1)
                for h in range(QPK):
                    last = pe.matmul(o_ps[32 * h:32 * (h + 1), q0:], vs[e][:, kb, :], probs[u % len(probs)][:, h, q0:],
                                     start=(u in CHUNK_FIRST), stop=(u in CHUNK_LAST))
                last.then_inc(pv_done, 1)

            def group(r, e, groups_left=GROUPS):
                r1, e1 = after(r, e)
                lent = None
                for u in range(SU):
                    for slot in range(3):
                        if slot < 2 and u + AHEAD < SU:
                            s_unit(r, e, u + AHEAD, slot)
                        elif slot < 2 and groups_left:
                            s_unit(r1, e1, u + AHEAD - SU, slot)
                        if slot == 2:
                            if u == SHIFT_AT[0] and groups_left:
                                lent = transpose_shift(r1, e1, 0, 2 * r1 + e1, LENT[0])
                            if u == SHIFT_AT[1] and groups_left:
                                lent = transpose_shift(r1, e1, 1, 2 * r1 + e1 + 1, LENT[1])
                            value_unit(r, e, u)
                        for ahead, m in M_AT[u][slot]:
                            if ahead <= groups_left:
                                m_unit(*((r1, e1) if ahead == 1 else (r + 1, e)), m, lent)
                                lent = None

            pe.sem_inc(pv_done, len(probs))
            lent = None
            for m in range(MU):
                if m == LENT_START[0]:
                    lent = transpose_shift(0, 0, 0, 0, m)
                m_unit(0, 0, m, lent)
                lent = None
            for m in range(M_FIRST):
                if m == M_FIRST - 1:
                    lent = transpose_shift(0, 0, 1, 1, m)
                m_unit(0, 1, m, lent)
            for u in range(AHEAD):
                s_unit(0, 0, u, 0)
                s_unit(0, 0, u, 1)
            with pe.Fori(0, ROUNDS - 1) as r:
                group(r, 0)
                group(r, 1)
            group(ROUNDS - 1, 0, groups_left=1)
            group(ROUNDS - 1, 1, groups_left=0)

        @block.vector
        def _(dve):
            def m_unit(r, e, m):
                t, h, kc, n = M_UNITS[m]
                wait_apart(dve, m_done, (2 * r + e) * MU + m + 1, passed)
                if kc == t // TPC:
                    dve.tensor_tensor_reduce(out=scratch[m % M_BANKS][:, :n], in0=m_ps[m % M_BANKS][:, :n], in1=causal[:, N - n:],
                                             scale=1.0, scalar=-3.0e38, op0=ALU.add, op1=ALU.max,
                                             accum_out=max_a[:, h, t:t + 1]).then_inc(m_taken, 1)
                else:
                    dve.tensor_reduce(max_b[:, h, t - TPC:t - TPC + 1], m_ps[m % M_BANKS][:, :n], mybir.AxisListType.X,
                                      ALU.max).then_inc(m_taken, 1)

            step = Steps(max_step, per_round=2 * (3 + 4))

            def split_maxima(r, e, qc):
                g = 2 * r + e
                step.n = (3 + 4) * e + 3 * qc
                dve.wait_ge(m_taken, g * MU + (MU if qc else MU_HALF))
                top = max_a[:, :, qc * TPC:(qc + 1) * TPC].rearrange("p h t -> p t h")
                if qc:
                    step.mark(dve.tensor_tensor(max_ab[:], top, max_b[:].rearrange("p h t -> p t h"), ALU.max))
                    dve.wait_ge(max_step, step.value(r))
                    top = max_ab[:]
                step.mark(dve.tensor_scalar(shift[qc][:, :, :, 0], top, -1.0, None, ALU.mult))
                dve.wait_ge(max_step, step.value(r))
                step.mark(dve.scalar_tensor_tensor(out=left[:], in0=top, scalar=-1.0, in1=shift[qc][:, :, :, 0],
                                                   op0=ALU.mult, op1=ALU.subtract))
                dve.wait_ge(max_step, step.value(r))
                step.mark(dve.tensor_copy(shift[qc][:, :, :, 1], left[:]))
                dve.wait_ge(max_step, step.value(r))
                dve.tensor_tensor(shift[qc][:, :, :, 2], left[:], shift[qc][:, :, :, 1], ALU.subtract)\
                   .then_inc(shift_ready, 1)

            def group(r, e):
                for m in range(MU):
                    m_unit(r, e, m)
                    if m == MU_HALF - 1:
                        split_maxima(r, e, 0)
                split_maxima(r, e, 1)

            for tile in (*mq, *mk, *sq):
                dve.memset(tile[:], 0.0).then_inc(zeros_ready, 1)
            dve.wait_ge(masks_ready, 2)
            with dve.Fori(0, ROUNDS) as r:
                group(r, 0)
                group(r, 1)

        @block.scalar
        def _(act):
            def exponentials(r, e, u):
                g = 2 * r + e
                n = g * SU + u
                _, _, q0 = S_UNITS[u]
                act.wait_ge(pv_done, n + 1)
                for pair in range(2):
                    act.wait_ge(s_done, 2 * n + pair + 1)
                    act.activation(probs[u % len(probs)][:, 2 * pair:2 * pair + 2, q0:], s_ps[pair][:, :, q0:], ACT.Exp,
                                   scale=SCALE).then_inc(exp_done, 1)

            def take_shift(r, e, qc, m):
                g = 2 * r + e
                act.wait_ge(t_done, QC * g + qc + 1)
                act.wait_ge(shift_loaded[qc], 16 * QPK * g)
                act.activation(shift_t[qc][:], t_ps[m % M_BANKS], ACT.Copy).then_inc(shift_t_ready, 1)

            def take_sums(r, e, qc):
                g = 2 * r + e
                act.wait_ge(pv_done, g * SU + CHUNK_LAST[qc] + 1 + len(probs))
                act.wait_ge(sums_stored[qc], 16 * g)
                act.activation(sums[qc][:], o_ps[:], ACT.Copy).then_inc(o_taken, 1)

            def store_sums(r, e, qc):
                act.wait_ge(o_taken, QC * (2 * r + e) + qc + 1)
                tile = e * KB + qc * TPC
                act.dma_start(sum_tiles[tile:tile + TPC, :, bass.ds(r, 1), :].rearrange("t p a n -> p t (a n)"),
                              sums[qc][:].rearrange("p (t n) -> p t n", n=P)).then_inc(sums_stored[qc], 16)

            def group(r, e, last=False):
                r1, e1 = after(r, e)
                for u in range(SU):
                    if u + AHEAD < SU:
                        exponentials(r, e, u + AHEAD)
                    elif not last:
                        exponentials(r1, e1, u + AHEAD - SU)
                    if u in SHIFT_AT and not last:
                        qc = SHIFT_AT.index(u)
                        take_shift(r1, e1, qc, LENT[qc])
                    if u in CHUNK_LAST:
                        take_sums(r, e, CHUNK_LAST.index(u))
                        store_sums(r, e, CHUNK_LAST.index(u))

            for qc in range(QC):
                take_shift(0, 0, qc, LENT_START[qc])
            for u in range(AHEAD):
                exponentials(0, 0, u)
            with act.Fori(0, ROUNDS - 1) as r:
                group(r, 0)
                group(r, 1)
            group(ROUNDS - 1, 0)
            group(ROUNDS - 1, 1, last=True)

        @block.gpsimd
        def _(pool):
            def mask(r, e, u):
                g = 2 * r + e
                _, _, q0 = S_UNITS[u]
                wait_apart(pool, exp_done, 2 * (g * SU + u) + 2, passed)
                blk = probs[u % len(probs)][:, :, q0:q0 + P]
                pool.affine_select(out=blk, in_=blk, compare_op=ALU.is_ge, fill=0.0, base=0,
                                   pattern=[[0, QPK], [1, P]], channel_multiplier=-1).then_inc(masked, 1)

            def stage_values(r, e):
                g = 2 * r + e
                pool.tensor_copy(vs[e][:, :, 0:HD], v.rearrange("p h (b k) d -> p (h b k) d", b=B)
                                 [:, bass.ds(g * KB, KB), :]).then_inc(v_staged, 1)

            def add_bias(r, e):
                tile = x[:, bass.ds(2 * r + e, 1), :].rearrange("p a c -> p (a c)")
                pool.tensor_tensor(tile, tile, bo[:], ALU.add).then_inc(x_biased, 1)

            def group(r, e, last=False):
                if not last:
                    pool.wait_ge(pv_done, (2 * r + e) * SU + len(probs))
                    stage_values(*after(r, e))
                for u in DIAGONAL:
                    mask(r, e, u)
                    if u == DIAGONAL[TPC - 1]:
                        add_bias(r, e)

            pool.memset(causal[:], 0.0).then_inc(masks_ready, 1)
            pool.wait_ge(masks_ready, 1)
            pool.affine_select(out=causal[:, N - P:], in_=causal[:, N - P:], compare_op=ALU.is_ge, fill=MASKED, base=0,
                               pattern=[[-1, P]], channel_multiplier=1).then_inc(masks_ready, 1)
            for e in range(2):
                pool.memset(sk[e][:], 1.0).then_inc(ones_ready, 1)
            for e in range(2):
                pool.memset(vs[e][:], 0.0).then_inc(ones_ready, 1)
            pool.wait_ge(ones_ready, 4)
            for e in range(2):
                pool.memset(vs[e][:, :, HD:HD + 1], 1.0).then_inc(ones_ready, 1)
            pool.wait_ge(ones_ready, 6)
            stage_values(0, 0)
            pool.wait_ge(bo_loaded, 16)
            with pool.Fori(0, ROUNDS - 1) as r:
                group(r, 0)
                group(r, 1)
            group(ROUNDS - 1, 0)
            group(ROUNDS - 1, 1, last=True)

        @block.sync
        def _(sp):
            q_groups = q_rows.rearrange("(g i d) r t -> g (d r) i t", i=QPK, d=HD)
            k_groups = k_rows.rearrange("(g d) r t -> g (d r) t", d=HD)
            LOADS = 2

            def load_m(r, e):
                tokens = slice(e * T, (e + 1) * T)
                sp.dma_start(mq[e][:ROWS], q_groups[bass.ds(r, 1), :, :, tokens]
                             .rearrange("g r i t -> r (g i) t")).then_inc(m_loaded[e], 16)
                sp.dma_start(mk[e][:ROWS], k_groups[bass.ds(r, 1), :, tokens]
                             .rearrange("g r t -> r (g t)")).then_inc(m_loaded[e], 16)

            def copy_s(r, e):
                sp.wait_ge(m_loaded[e], 16 * LOADS * (r + 1))
                sp.dma_start(sq[e][:ROWS], mq[e][:ROWS]).then_inc(s_loaded[e], 16)
                sp.dma_start(sk[e][:ROWS], mk[e][:ROWS]).then_inc(s_loaded[e], 16)

            def load_shift(r, e, qc):
                sp.wait_ge(shift_t_ready, QC * (2 * r + e) + qc + 1)
                for h in range(QPK):
                    sp.dma_start(sq[e][ROWS:ROWS + SHIFT, h, qc * N:(qc + 1) * N],
                                 shift_t[qc][h * SHIFT:(h + 1) * SHIFT, :]).then_inc(shift_loaded[qc], 16)

            def next_m(r, e):
                sp.wait_ge(s_loaded[e], 16 * LOADS * (r + 1))
                sp.wait_ge(m_done, MU * (2 * r + e + 1))
                load_m(r + 1, e)

            def group(r, e, loads=True, last=False):
                r1, e1 = after(r, e)
                if not last:
                    sp.wait_ge(s_done, 2 * SU * (2 * r + e))
                    copy_s(r1, e1)
                    load_shift(r1, e1, 0)
                    load_shift(r1, e1, 1)
                if loads:
                    next_m(r1, e1)

            sp.dma_start(bo[:], bo_row.partition_broadcast(P)).then_inc(bo_loaded, 16)
            sp.wait_ge(zeros_ready, 6)
            load_m(0, 0)
            load_m(0, 1)
            sp.wait_ge(ones_ready, 2)
            copy_s(0, 0)
            load_shift(0, 0, 0)
            load_shift(0, 0, 1)
            next_m(0, 0)
            with sp.Fori(0, ROUNDS - 2) as r:
                group(r, 0)
                group(r, 1)
            group(ROUNDS - 2, 0)
            group(ROUNDS - 2, 1, loads=False)
            group(ROUNDS - 1, 0, loads=False)
            group(ROUNDS - 1, 1, loads=False, last=True)
            for qc in range(QC):
                sp.wait_ge(sums_stored[qc], 16 * GROUPS)
            sp.wait_ge(x_biased, GROUPS)


def output_phase(nc, sum_tiles, wo, ident, x, HD):
    _, TILES, C = x.shape
    KT = C // P
    KVH = sum_tiles.shape[2]
    HPK = C // HD // KVH
    with ExitStack() as ctx:
        def sb(name, shape, dt):
            return [ctx.enter_context(nc.sbuf_tensor(f"out_{name}{e}", shape, dt)) for e in range(2)]

        def pb(name, shape):
            return [ctx.enter_context(nc.psum_tensor(f"out_{name}{e}", shape, F32)) for e in range(2)]

        def sem(name):
            return ctx.enter_context(nc.semaphore(f"out_{name}"))

        sums = sb("sums", [P, KVH, P], F32)
        inverse = sb("inverse", [P, KVH * HPK, 1], F32)
        attn = sb("attn", [P, KVH * HPK, HD], F32)
        at_hi = sb("at_hi", [P, KT, P], F32R)
        at_lo = sb("at_lo", [P, KT, P], F32R)
        sums_ps = pb("sums_ps", [P, KVH, P])
        at_ps = pb("at_ps", [P, KT, P])
        y_ps = pb("y_ps", [P, C])

        loaded = [sem(f"loaded{e}") for e in range(2)]
        sums_done = sem("sums_done")
        inverse_ready = sem("inverse_ready")
        attn_ready = sem("attn_ready")
        at_done = sem("at_done")
        hi_ready = sem("hi_ready")
        lo_ready = sem("lo_ready")
        y_done = sem("y_done")
        y_added = sem("y_added")
        block = ctx.enter_context(nc.Block())
        ROUNDS = TILES // 2

        def skewed(engine, steps):
            S = len(steps) - 1
            FIRST = (S + 3) // 2

            def tile(r, n, low=0, high=len(steps)):
                for k in range(low, high):
                    steps[k](r + (n - k) // 2, (n - k) % 2)

            for n in range(2 * FIRST):
                tile(0, n, high=min(n, S) + 1)
            with engine.Fori(FIRST, ROUNDS) as r:
                tile(r, 0)
                tile(r, 1)
            for n in range(S):
                tile(ROUNDS, n, low=n + 1)

        def before(engine, signal, r, e):
            if not (isinstance(r, int) and r < 1):
                engine.wait_ge(signal, 2 * r + e - 1)

        @block.sync
        def _(sp):
            def load(r, e):
                before(sp, sums_done, r, e)
                sp.dma_start(sums[e][:], sum_tiles[bass.ds(2 * r + e, 1)].rearrange("a p h n -> p (a h) n"))\
                  .then_inc(loaded[e], 16)

            skewed(sp, [load])
            sp.wait_ge(y_added, TILES)

        @block.tensor
        def _(pe):
            def transpose_sums(r, e):
                pe.wait_ge(loaded[e], 16 * (r + 1))
                before(pe, attn_ready, r, e)
                for h in range(KVH):
                    last = pe.transpose(sums_ps[e][:, h, :], sums[e][:, h, :], ident[:])
                last.then_inc(sums_done, 1)

            def transpose_attn(r, e):
                pe.wait_ge(attn_ready, 2 * r + e + 1)
                before(pe, lo_ready, r, e)
                flat = attn[e][:].rearrange("p h d -> p (h d)")
                for k in range(KT):
                    last = pe.transpose(at_ps[e][:, k, :], flat[:, k * P:(k + 1) * P], ident[:])
                last.then_inc(at_done, 1)

            def project(r, e):
                pe.wait_ge(hi_ready, 2 * r + e + 1)
                pe.wait_ge(lo_ready, 2 * r + e + 1)
                before(pe, y_added, r, e)
                i = 0
                for k in range(KT):
                    for hs, ws in ((at_hi[e], wo[0]), (at_hi[e], wo[1]), (at_lo[e], wo[0])):
                        last = pe.matmul(y_ps[e][:], hs[:, k, :], ws[:, k, :], start=(i == 0), stop=(i == 3 * KT - 1))
                        i += 1
                last.then_inc(y_done, 1)

            skewed(pe, [transpose_sums, transpose_attn, project])

        @block.scalar
        def _(act):
            def high_part(r, e):
                act.wait_ge(at_done, 2 * r + e + 1)
                before(act, y_done, r, e)
                act.activation(at_hi[e][:], at_ps[e][:], ACT.Copy).then_inc(hi_ready, 1)

            skewed(act, [high_part])

        @block.vector
        def _(dve):
            def divide(r, e):
                dve.wait_ge(sums_done, 2 * r + e + 1)
                before(dve, at_done, r, e)
                rows = sums_ps[e][:].rearrange("p g (j d) -> p (g j) d", j=HPK)
                dve.reciprocal(inverse[e][:], rows[:, :, HD:HD + 1]).then_inc(inverse_ready, 1)
                dve.wait_ge(inverse_ready, 2 * r + e + 1)
                dve.tensor_tensor(attn[e][:], rows[:, :, 0:HD], inverse[e][:].to_broadcast([P, KVH * HPK, HD]),
                                  ALU.mult).then_inc(attn_ready, 1)

            def low_part(r, e):
                dve.wait_ge(hi_ready, 2 * r + e + 1)
                dve.tensor_tensor(at_lo[e][:], at_ps[e][:], at_hi[e][:].bitcast(F32), ALU.subtract).then_inc(lo_ready, 1)

            def add(r, e):
                dve.wait_ge(y_done, 2 * r + e + 1)
                tile = x[:, bass.ds(2 * r + e, 1), :].rearrange("p a c -> p (a c)")
                dve.tensor_tensor(tile, y_ps[e][:], tile, ALU.add).then_inc(y_added, 1)

            skewed(dve, [divide, low_part, add])


def load_phase(nc, x, x_rows, ident, ident_bf, splits, x_loaded, ident_ready, weights_ready):
    with ExitStack() as ctx:
        raws = [ctx.enter_context(nc.sbuf_tensor(f"raw{n}", shape, F32)) for n, (_, shape, _) in enumerate(splits)]
        loaded = [ctx.enter_context(nc.semaphore(f"raw_loaded{n}")) for n in range(len(splits))]
        hi_done = ctx.enter_context(nc.semaphore("w_hi_done"))
        lo_done = ctx.enter_context(nc.semaphore("w_lo_done"))
        block = ctx.enter_context(nc.Block())
        pieces = [(n, read(raw), hi, lo) for n, (raw, (_, _, ps)) in enumerate(zip(raws, splits)) for read, hi, lo in ps]

        @block.sync
        def _(sp):
            sp.dma_start(x[:], x_rows).then_inc(x_loaded, 16)
            for raw, (rows, _, _), sem in zip(raws, splits, loaded):
                sp.dma_start(raw[:], rows).then_inc(sem, 16)

        @block.gpsimd
        def _(pool):
            make_identity(pool, ident, ident_ready)
            pool.wait_ge(ident_ready, 2)
            pool.tensor_copy(ident_bf[:], ident[:]).then_inc(ident_ready, 1)

        @block.scalar
        def _(act):
            for n, src, hi, _ in pieces:
                act.wait_ge(loaded[n], 16)
                act.activation(hi, src, ACT.Copy).then_inc(hi_done, 1)

        @block.vector
        def _(dve):
            for i, (n, src, hi, lo) in enumerate(pieces):
                dve.wait_ge(hi_done, i + 1)
                dve.tensor_tensor(lo, src, hi.bitcast(F32), ALU.subtract).then_inc(lo_done, 1)
            dve.wait_ge(lo_done, len(pieces))
            dve.wait_ge(ident_ready, 3)
            dve.sem_inc(weights_ready, 1)


def build(nc, x_in, w_qkv, bias_cols, bv, w_o, bo, w_gate, w_up, w_down, cos_t, sin_t, out, HD=8, SPLIT=9):
    B, T, C = x_in.shape
    TILES = B * T // P
    HID = w_gate.shape[1]
    KT, BLKS, J = C // P, HID // 512, 4
    KV = bv.shape[0]
    KVH = KV // HD
    with ExitStack() as ctx:
        def sb(name, shape, dt, on=ctx):
            return on.enter_context(nc.sbuf_tensor(name, shape, dt))

        def sem(name):
            return ctx.enter_context(nc.semaphore(name))

        x = sb("x", [P, TILES, C], F32)
        ident = sb("ident", [P, P], F32)
        ident_bf = sb("ident_bf", [P, P], BF16)
        parts = ("hi", "lo")
        wg = [sb(f"wg_{n}", [P, KT, BLKS, J, P], F32R) for n in parts]
        wu = [sb(f"wu_{n}", [P, KT, BLKS, J, P], F32R) for n in parts]
        wd = [sb(f"wd_{n}", [P, BLKS, J, C], F32R) for n in parts]
        wo = [sb(f"wo_{n}", [P, KT, C], F32R) for n in parts]
        v = sb("v", [P, KVH, TILES, HD], F32)
        until_qkv = ctx.enter_context(ExitStack())
        wqkv = [sb(f"wqkv_{n}", [P, KT, w_qkv.shape[1]], F32R, until_qkv) for n in parts]
        x_loaded, ident_ready, weights_ready = sem("x_loaded"), sem("ident_ready"), sem("weights_ready")
        x_rows = x_in.rearrange("b (t p) c -> p (b t) c", p=P)
        out_rows = out.rearrange("b (t p) c -> p (b t) c", p=P)
        q_rows = nc.dram_tensor("q_rows", [C, SPLIT, B * T], BF16).ap()
        sum_tiles = nc.dram_tensor("sum_tiles", [TILES, P, KVH, P], F32).ap()
        k_rows = nc.dram_tensor("k_rows", [KV, SPLIT, B * T], BF16).ap()

        def by_blocks(w):
            return [(lambda raw, k=k, b=b: raw[:, k, b * 512:(b + 1) * 512].rearrange("q (p j) -> q j p", j=J),
                     w[0][:, k, b], w[1][:, k, b]) for b in range(BLKS) for k in range(KT)]

        def whole(w):
            return [(lambda raw: raw[:], w[0][:], w[1][:])]

        splits = [(w_gate.rearrange("(k p) n -> p k n", p=P), [P, KT, HID], by_blocks(wg)),
                  (w_up.rearrange("(k p) n -> p k n", p=P), [P, KT, HID], by_blocks(wu)),
                  (w_down.rearrange("(b p j) c -> p b j c", p=P, j=J), [P, BLKS, J, C], whole(wd)),
                  (w_qkv.rearrange("(k p) n -> p k n", p=P), [P, KT, w_qkv.shape[1]], whole(wqkv)),
                  (w_o.rearrange("(k p) n -> p k n", p=P), [P, KT, C], whole(wo))]
        load_phase(nc, x, x_rows, ident, ident_bf, splits, x_loaded, ident_ready, weights_ready)
        ffn_phase(nc, "ffn1", x, (wg, wu, wd), ident, weights_ready, x_loaded, None)
        qkv_phase(nc, x, ident, wqkv, bias_cols, bv, cos_t, sin_t, q_rows, k_rows, v)
        until_qkv.close()
        attention_phase(nc, q_rows, k_rows, v, sum_tiles, ident_bf, x, bo, T, HD)
        output_phase(nc, sum_tiles, wo, ident, x, HD)
        ffn_phase(nc, "ffn2", x, (wg, wu, wd), ident, weights_ready, x_loaded, out_rows)


def rope_tables(T, B, HD):
    import numpy as np

    inverse = (1.0 / np.float32(ROPE_BASE) ** (np.arange(0, HD, 2, dtype=np.float32) / np.float32(HD))).astype(np.float32)
    angles = np.outer(np.arange(T, dtype=np.float32), inverse).astype(np.float32)
    cos = np.repeat(np.cos(angles), 2, axis=1).T
    sin = np.repeat(np.sin(angles), 2, axis=1).T * np.tile(np.array([[-1.0], [1.0]], np.float32), (HD // 2, 1))
    return (np.ascontiguousarray(np.tile(cos, (P // HD, B)), dtype=np.float32),
            np.ascontiguousarray(np.tile(sin, (P // HD, B)), dtype=np.float32))


def swapped(a):
    return a.reshape(*a.shape[:-1], -1, 2)[..., ::-1].reshape(a.shape)


def kernel(**inputs):
    import numpy as np
    import concourse.bacc as bacc
    from concourse.bass_utils import run_bass_kernel_spmd

    a = {name.split("_", 1)[1]: np.asarray(value) for name, value in inputs.items()}
    x = a["attn_x"]
    B, T, C = x.shape
    HD = 8
    wq, wk, bq, bk = a["attn_Wq"], a["attn_Wk"], a["attn_bq"], a["attn_bk"]
    tiles = [wq[:, :P], wq[:, P:], np.concatenate([wk, wk], axis=1)]
    w_qkv = np.concatenate([w for t in tiles for w in (t, swapped(t))] + [a["attn_Wv"]], axis=1)
    b_tiles = [bq[:P], bq[P:], np.concatenate([bk, bk])]
    bias_cols = np.stack([b for t in b_tiles for b in (t, swapped(t))], axis=1)
    cos_t, sin_t = rope_tables(T, B, HD)
    arrays = {"x": x, "w_qkv": w_qkv, "bias_cols": bias_cols, "bv": a["attn_bv"], "w_o": a["attn_Wo"], "bo": a["attn_bo"],
              "w_gate": a["ffn_w_gate"], "w_up": a["ffn_w_up"], "w_down": a["ffn_w_down"], "cos_t": cos_t, "sin_t": sin_t}
    nc = bacc.Bacc("TRN2", target_bir_lowering=False, num_devices=1)
    arrays = {f"in_{name}": np.ascontiguousarray(value) for name, value in arrays.items()}
    args = [nc.dram_tensor(name, value.shape, mybir.dt.from_np(value.dtype), kind="ExternalInput").ap()
            for name, value in arrays.items()]
    out = nc.dram_tensor("out", x.shape, F32, kind="ExternalOutput").ap()
    build(nc, *args, out)
    result = run_bass_kernel_spmd(nc, [arrays], core_ids=[0])
    return result.results[0]["out"]
```

```python
import concourse.bass as bass
from concourse import mybir
from collections import namedtuple
from contextlib import ExitStack

F32 = mybir.dt.float32
F32R = mybir.dt.float32r
BF16 = mybir.dt.bfloat16
ALU = mybir.AluOpType
ACT = mybir.ActivationFunctionType

P = 128
EPS = 1e-5
ROPE_BASE = 10000.0
MASKED = -1.0e30
LOWEST = -3.0e38


class Steps:

    def __init__(self, sem, per_round):
        self.sem, self.per_round, self.n = sem, per_round, 0

    def mark(self, instruction):
        self.n += 1
        return instruction.then_inc(self.sem, 1)

    def value(self, round_index):
        return self.n + self.per_round * round_index


def wait_apart(engine, sem, value, passed):
    engine.wait_ge(sem, value)
    engine.sem_inc(passed, 1)


def make_identity(pool, ident, signal):
    pool.memset(ident[:], 0.0).then_inc(signal, 1)
    pool.wait_ge(signal, 1)
    pool.affine_select(out=ident[:], in_=ident[:], compare_op=ALU.not_equal, fill=1.0, base=0,
                       pattern=[[-1, P]], channel_multiplier=1).then_inc(signal, 1)


class NormedChunks:

    def __init__(self, nc, ctx, tag, x, ident, N, keep_all=False):
        self.keep_all = keep_all
        _, self.TILES, self.C = x.shape
        self.x, self.ident, self.N = x, ident, N
        self.TPC = N // P
        self.KT = self.C // P
        TPC, C, KT = self.TPC, self.C, self.KT

        def sb(name, shape, dt):
            return ctx.enter_context(nc.sbuf_tensor(f"{tag}_{name}", shape, dt))

        def sem(name):
            return ctx.enter_context(nc.semaphore(f"{tag}_{name}"))

        self.stats = sb("stats", [P, TPC, 6], F32)
        kept = self.TILES if keep_all else TPC
        self.mean_var = sb("mean_var", [P, kept, 2], F32)
        self.var_eps = sb("var_eps", [P, kept], F32)
        self.rstd = sb("rstd", [P, kept], F32)
        self.minus_half = sb("minus_half", [P, TPC], F32)
        self.xn = sb("xn", [P, TPC, C], F32)
        self.xt_hi = sb("xt_hi", [P, KT, N], F32R)
        self.xt_lo = sb("xt_lo", [P, KT, N], F32R)
        self.xt_ps = ctx.enter_context(nc.psum_tensor(f"{tag}_xt_ps", [P, KT, N], F32))
        self.passed = sem("passed")
        self.stats_step = sem("stats_step")
        self.stats_ready = sem("stats_ready")
        self.var_ready = sem("var_ready")
        self.rstd_ready = sem("rstd_ready")
        self.xn_ready = sem("xn_ready")
        self.xt_done = sem("xt_done")
        self.hi_ready = sem("xt_hi_ready")
        self.lo_ready = sem("xt_lo_ready")
        self.xt_used = sem("xt_used")

    def kept(self, c, t, tiles=1):
        return bass.ds(c * self.TPC + t, tiles) if self.keep_all else slice(t, t + tiles)

    def x_tile(self, c, t):
        return self.x[:, bass.ds(c * self.TPC + t, 1), :].rearrange("p a c -> p (a c)")

    def statistics(self, dve, c):
        if self.keep_all and c:
            dve.wait_ge(self.stats_ready, c)
        for t in range(self.TPC):
            dve.bn_stats(self.stats[:, t, :], self.x_tile(c, t)).then_inc(self.stats_step, 1)
        for t in range(self.TPC):
            wait_apart(dve, self.stats_step, c * self.TPC + t + 1, self.passed)
            last = dve.bn_aggr(self.mean_var[:, self.kept(c, t), :].rearrange("p a c -> p (a c)"),
                               self.stats[:, t, :])
        last.then_inc(self.stats_ready, 1)

    def exponents(self, pool):
        pool.memset(self.minus_half[:], -0.5).then_inc(self.var_ready, 1)

    def inverse_deviation(self, pool, c):
        wait_apart(pool, self.stats_ready, c + 1, self.passed)
        tiles = self.kept(c, 0, self.TPC)
        pool.tensor_scalar(self.var_eps[:, tiles], self.mean_var[:, tiles, 1], EPS, None, ALU.add).then_inc(self.var_ready, 1)
        pool.wait_ge(self.var_ready, c + 2)
        pool.tensor_tensor(self.rstd[:, tiles], self.var_eps[:, tiles], self.minus_half[:], ALU.pow).then_inc(self.rstd_ready, 1)

    def normalise(self, dve, c):
        dve.wait_ge(self.rstd_ready, c + 1)
        for t in range(self.TPC):
            tile = self.kept(c, t)
            last = dve.tensor_scalar(self.xn[:, t, :], self.x_tile(c, t), self.mean_var[:, tile, 0],
                                     self.rstd[:, tile], ALU.subtract, ALU.mult)
        last.then_inc(self.xn_ready, 1)

    def transpose(self, pe, c):
        pe.wait_ge(self.xn_ready, c + 1)
        for t in range(self.TPC):
            for k in range(self.KT):
                last = pe.transpose(self.xt_ps[:, k, t * P:(t + 1) * P], self.xn[:, t, k * P:(k + 1) * P],
                                    self.ident[:])
        last.then_inc(self.xt_done, 1)

    def high_parts(self, act, c, k):
        act.wait_ge(self.xt_done, c + 1)
        act.activation(self.xt_hi[:, k, :], self.xt_ps[:, k, :], ACT.Copy).then_inc(self.hi_ready, 1)

    def low_parts(self, dve, c, k):
        dve.wait_ge(self.hi_ready, c * self.KT + k + 1)
        dve.tensor_tensor(self.xt_lo[:, k, :], self.xt_ps[:, k, :], self.xt_hi[:, k, :].bitcast(F32), ALU.subtract)\
           .then_inc(self.lo_ready, 1)

    def wait_split(self, pe, c, k):
        pe.wait_ge(self.hi_ready, c * self.KT + k + 1)
        pe.wait_ge(self.lo_ready, c * self.KT + k + 1)


XLoads = namedtuple("XLoads", "pieces ident_ready ident_bf raw")


class WeightLoads:

    def __init__(self, nc, ctx, tag, loads):
        self.loads = loads
        self.loaded = [ctx.enter_context(nc.semaphore(f"{tag}_loaded{n}")) for n in range(len(loads))]
        self.hi_ready = ctx.enter_context(nc.semaphore(f"{tag}_w_hi_ready"))
        self.ready = ctx.enter_context(nc.semaphore(f"{tag}_w_ready"))

    def high_parts(self, act, n):
        _, _, loaded, hi, _ = self.loads[n]
        act.wait_ge(self.loaded[n], 16)
        act.activation(hi, loaded, ACT.Copy).then_inc(self.hi_ready, 1)

    def low_parts(self, dve, n):
        _, _, loaded, hi, lo = self.loads[n]
        dve.wait_ge(self.hi_ready, n + 1)
        dve.tensor_tensor(lo, loaded, hi.bitcast(F32), ALU.subtract).then_inc(self.ready, 1)

    def load(self, sp, n):
        dram, tile, *_ = self.loads[n]
        sp.dma_start(tile, dram).then_inc(self.loaded[n], 16)


def ffn_phase(nc, tag, x, weights, ident, first_loads=None, out_rows=None):
    _, TILES, C = x.shape
    KT = C // P
    wg, wu, wd = weights
    BLKS = wd[0].shape[1]
    J = 4
    N = 512
    TPC = N // P
    CHUNKS = TILES // TPC
    SPARSIFY_STEPS = 10
    assert BLKS == 2 and CHUNKS >= 3

    with ExitStack() as ctx:
        def sb(name, shape, dt):
            return ctx.enter_context(nc.sbuf_tensor(f"{tag}_{name}", shape, dt))

        def pb(name, shape, dt=F32):
            return ctx.enter_context(nc.psum_tensor(f"{tag}_{name}", shape, dt))

        def sem(name):
            return ctx.enter_context(nc.semaphore(f"{tag}_{name}"))

        normed = NormedChunks(nc, ctx, tag, x, ident, N)
        silu = sb("silu", [P, 2, N], F32)
        h = sb("h", [P, BLKS, J, N], F32)
        a = sb("a", [P, BLKS, J, N], F32)
        pair_max = sb("pair_max", [P, 2, N], F32)
        pair_min = sb("pair_min", [P, 2, N], F32)
        first_wins = sb("first_wins", [P, 2, N], BF16)
        both_low = sb("both_low", [P, N], BF16)
        both_high = sb("both_high", [P, N], BF16)
        tilt = sb("tilt", [P, N], BF16)
        rank = sb("rank", [P, J, N], BF16)
        hs = sb("hs", [P, J, N], F32)
        hs_hi = sb("hs_hi", [P, BLKS, J, N], F32R)
        hs_lo = sb("hs_lo", [P, BLKS, J, N], F32R)

        gu = [[pb(f"{w}{i}", [P, N]) for w in ("gate", "up")] for i in range(2)]
        y_ps = pb("y_ps", [P, TPC, C])

        gu_done = sem("gu_done")
        silu_ready = sem("silu_ready")
        h_ready = sem("h_ready")
        abs_ready = sem("abs_ready")
        dve_step = sem("dve_step")
        hs_ready = sem("hs_ready")
        hi_ready = sem("hi_ready")
        lo_ready = sem("lo_ready")
        hs_free = sem("hs_free")
        y_done = sem("y_done")
        y_added = sem("y_added")
        stored = sem("stored")
        if first_loads:
            x_loads, w_loads = first_loads
            x_loaded = [sem(f"x_loaded{n}") for n in range(len(x_loads))]

        block = ctx.enter_context(nc.Block())

        def before(c, blk):
            return (c, 0) if blk else (c - 1, 1)

        @block.tensor
        def _(pe):
            def gate_up(c, blk, j, first):
                i = j % 2
                if not (first and j < 2):
                    pe.wait_ge(h_ready, (c * BLKS + blk) * J + j - 1)
                for k in range(KT):
                    if blk == 0 and j == 0:
                        normed.wait_split(pe, c, k)
                    for w, ps in zip((wg, wu), gu[i]):
                        for n, (ws, xs) in enumerate(((w[0], normed.xt_hi), (w[1], normed.xt_hi), (w[0], normed.xt_lo))):
                            last = pe.matmul(ps[:], ws[:, k, blk, j, :], xs[:, k, :],
                                             start=(k == 0 and n == 0), stop=(k == KT - 1 and n == 2))
                    if k == KT - 1:
                        last.then_inc(gu_done, 1)
                    elif k == 0 and blk == BLKS - 1 and j == J - 1:
                        last.then_inc(normed.xt_used, 1)

            def down(c, blk, j):
                if blk == 0 and j == 0:
                    pe.wait_ge(y_added, c)
                n = (c * BLKS + blk) * J + j + 1
                pe.wait_ge(hi_ready, n)
                pe.wait_ge(lo_ready, n)
                for t in range(TPC):
                    rows = slice(t * P, (t + 1) * P)
                    for m, (hp, wp) in enumerate(((hs_hi, wd[0]), (hs_hi, wd[1]), (hs_lo, wd[0]))):
                        last = pe.matmul(y_ps[:, t, :], hp[:, blk, j, rows], wp[:, blk, j, :],
                                         start=(blk == 0 and j == 0 and m == 0 and t % 2 == 0),
                                         stop=(blk == BLKS - 1 and j == J - 1 and m == 2),
                                         skip_group_check=True)
                if j == J - 1:
                    last.then_inc(hs_free, 1)
                    if blk == BLKS - 1:
                        pe.drain().then_inc(y_done, 1)

            def stage(c, blk, hidden=True, multiply=True, first=False, more=True):
                for j in range(J):
                    if hidden:
                        gate_up(c, blk, j, first)
                        if blk == 1 and j == 1 and more:
                            normed.transpose(pe, c + 1)
                    if multiply:
                        down(c - 1, blk, j)

            pe.sem_inc(hs_free, BLKS)
            if first_loads:
                pe.wait_ge(x_loads.ident_ready, 3)
            normed.transpose(pe, 0)
            if first_loads:
                pe.wait_ge(w_loads.ready, 2)
            stage(0, 0, multiply=False, first=True)
            if first_loads:
                pe.wait_ge(w_loads.ready, 4)
            stage(0, 1, multiply=False)
            if first_loads:
                pe.wait_ge(w_loads.ready, 6)
            with pe.Fori(1, CHUNKS - 1) as c:
                stage(c, 0)
                stage(c, 1)
            stage(CHUNKS - 1, 0)
            stage(CHUNKS - 1, 1, more=False)
            stage(CHUNKS, 0, hidden=False)
            stage(CHUNKS, 1, hidden=False)

        @block.scalar
        def _(act):
            def high_part(c, blk, j):
                if j == 0:
                    act.wait_ge(hs_free, c * BLKS + blk + 1)
                act.wait_ge(hs_ready, (c * BLKS + blk) * J + j + 1)
                act.activation(hs_hi[:, blk, j, :], hs[:, j, :], ACT.Copy).then_inc(hi_ready, 1)

            def stage(c, blk, hidden=True, sparse=True, more=True, extra=()):
                for j in range(J):
                    n = (c * BLKS + blk) * J + j + 1
                    turn = hidden and more and blk == 1 and j == J - 1
                    if turn:
                        act.wait_ge(normed.xt_used, c + 1)
                        normed.high_parts(act, c + 1, 0)
                    if hidden:
                        act.wait_ge(gu_done, n)
                    if turn:
                        for k in range(1, KT):
                            normed.high_parts(act, c + 1, k)
                    if hidden:
                        act.activation(silu[:, j % 2, :], gu[j % 2][0][:], ACT.Silu).then_inc(silu_ready, 1)
                    if sparse and j == J - 1:
                        high_part(*before(c, blk), 0)
                    if hidden:
                        act.wait_ge(h_ready, n)
                        act.activation(a[:, blk, j, :], h[:, blk, j, :], ACT.Abs).then_inc(abs_ready, 1)
                if sparse:
                    for j in range(1, J):
                        high_part(*before(c, blk), j)

            if first_loads:
                w_loads.high_parts(act, 0)
                w_loads.high_parts(act, 1)
            for k in range(KT):
                normed.high_parts(act, 0, k)
            if first_loads:
                for n in range(2, len(w_loads.loads)):
                    w_loads.high_parts(act, n)
            stage(0, 0, sparse=False)
            stage(0, 1)
            with act.Fori(1, CHUNKS - 1) as c:
                stage(c, 0)
                stage(c, 1)
            stage(CHUNKS - 1, 0)
            stage(CHUNKS - 1, 1, more=False)
            stage(CHUNKS, 0, hidden=False)

        @block.vector
        def _(dve):
            def sparsify(c, blk, part):
                b = c * BLKS + blk
                ab = a[:, blk]

                def mark(instruction):
                    instruction.then_inc(dve_step, 1)

                def wait_step(n):
                    dve.wait_ge(dve_step, b * SPARSIFY_STEPS + n)

                if part == 0:
                    dve.wait_ge(abs_ready, (b + 1) * J)
                    mark(dve.tensor_tensor(pair_max[:], ab[:, 0::2, :], ab[:, 1::2, :], ALU.max))
                    mark(dve.tensor_tensor(pair_min[:], ab[:, 0::2, :], ab[:, 1::2, :], ALU.min))
                if part == 1:
                    mark(dve.tensor_tensor(first_wins[:], ab[:, 0::2, :], ab[:, 1::2, :], ALU.is_ge))
                    wait_step(2)
                    mark(dve.tensor_tensor(both_low[:], pair_min[:, 0, :], pair_max[:, 1, :], ALU.is_ge))
                    mark(dve.tensor_tensor(both_high[:], pair_min[:, 1, :], pair_max[:, 0, :], ALU.is_gt))
                if part == 2:
                    wait_step(5)
                    mark(dve.tensor_tensor(tilt[:], both_low[:], both_high[:], ALU.subtract))
                    wait_step(6)
                    for j, op in enumerate((ALU.add, ALU.subtract, ALU.subtract, ALU.add)):
                        mark(dve.tensor_tensor(rank[:, j, :], first_wins[:, j // 2, :], tilt[:], op))
                    dve.wait_ge(hi_ready, b * J)
                    dve.wait_ge(lo_ready, b * J)
                for j in {2: (0,), 3: (1, 2, 3)}.get(part, ()):
                    keep(c, blk, j)

            def keep(c, blk, j):
                op, bound = (ALU.is_le, 0.0) if j % 2 else (ALU.is_ge, 1.0)
                dve.wait_ge(dve_step, (c * BLKS + blk) * SPARSIFY_STEPS + 7 + j)
                dve.scalar_tensor_tensor(out=hs[:, j, :], in0=rank[:, j, :], scalar=bound, in1=h[:, blk, j, :],
                                         op0=op, op1=ALU.mult).then_inc(hs_ready, 1)

            def add_down(c):
                dve.wait_ge(y_done, c + 1)
                rows = x[:, bass.ds(c * TPC, TPC), :].rearrange("p t c -> p (t c)")
                dve.scalar_tensor_tensor(out=rows, in0=y_ps[:].rearrange("p t c -> p (t c)"), scalar=0.5, in1=rows,
                                         op0=ALU.mult, op1=ALU.add).then_inc(y_added, 1)

            def stage(c, blk, hidden=True, sparse=True, add=True, more=True, extra={}):
                for j in range(J):
                    if blk == 0 and j == 0 and add:
                        add_down(c - 2)
                    if hidden:
                        if blk == 1 and j == J - 1 and more:
                            for k in range(KT):
                                normed.low_parts(dve, c + 1, k)
                        dve.wait_ge(silu_ready, (c * BLKS + blk) * J + j + 1)
                        dve.tensor_tensor(h[:, blk, j, :], gu[j % 2][1][:], silu[:, j % 2, :], ALU.mult).then_inc(h_ready, 1)
                    if sparse:
                        sparsify(*before(c, blk), j)
                    if blk == 0 and more and hidden:
                        if j == 1:
                            if first_loads and isinstance(c, int) and c == 0:
                                dve.wait_ge(x_loaded[1], 16)
                            normed.statistics(dve, c + 1)
                        if j == J - 1:
                            normed.normalise(dve, c + 1)
                    if j in extra:
                        w_loads.low_parts(dve, extra[j])

            if first_loads:
                dve.wait_ge(x_loaded[0], 16)
            normed.statistics(dve, 0)
            if first_loads:
                w_loads.low_parts(dve, 0)
            normed.normalise(dve, 0)
            if first_loads:
                w_loads.low_parts(dve, 1)
            for k in range(KT):
                normed.low_parts(dve, 0, k)
            stage(0, 0, sparse=False, add=False, extra={0: 2, 1: 3, 2: 4, 3: 5} if first_loads else {})
            stage(0, 1)
            stage(1, 0, add=False)
            stage(1, 1)
            with dve.Fori(2, CHUNKS - 1) as c:
                stage(c, 0)
                stage(c, 1)
            stage(CHUNKS - 1, 0, more=False)
            stage(CHUNKS - 1, 1, more=False)
            def last_low_part(j):
                dve.wait_ge(hi_ready, (CHUNKS * BLKS - 1) * J + j + 1)
                dve.tensor_tensor(hs_lo[:, 1, j, :], hs[:, j, :], hs_hi[:, 1, j, :].bitcast(F32), ALU.subtract).then_inc(lo_ready, 1)

            add_down(CHUNKS - 2)
            for part in range(3):
                sparsify(CHUNKS - 1, 1, part)
            for j in range(1, J):
                keep(CHUNKS - 1, 1, j)
                last_low_part(j - 1)
            last_low_part(J - 1)
            add_down(CHUNKS - 1)

        @block.gpsimd
        def _(pool):
            def low_parts(c, blk):
                pool.wait_ge(hs_free, c * BLKS + blk + 1)
                for j in range(J):
                    pool.wait_ge(hi_ready, (c * BLKS + blk) * J + j + 1)
                    pool.tensor_tensor(hs_lo[:, blk, j, :], hs[:, j, :], hs_hi[:, blk, j, :].bitcast(F32),
                                       ALU.subtract).then_inc(lo_ready, 1)

            normed.exponents(pool)
            if first_loads:
                make_identity(pool, ident, x_loads.ident_ready)
                pool.wait_ge(x_loads.ident_ready, 2)
                pool.tensor_copy(x_loads.ident_bf[:], ident[:]).then_inc(x_loads.ident_ready, 1)
            normed.inverse_deviation(pool, 0)
            normed.inverse_deviation(pool, 1)
            low_parts(0, 0)
            with pool.Fori(1, CHUNKS - 1) as c:
                normed.inverse_deviation(pool, c + 1)
                low_parts(c - 1, 1)
                low_parts(c, 0)
            low_parts(CHUNKS - 2, 1)
            low_parts(CHUNKS - 1, 0)

        @block.sync
        def _(sp):
            if first_loads:
                sp.dma_start(x_loads.pieces[0][0], x_loads.pieces[0][1]).then_inc(x_loaded[0], 16)
                for n in range(len(w_loads.loads)):
                    if n == 4:
                        sp.dma_start(x_loads.pieces[1][0], x_loads.pieces[1][1]).then_inc(x_loaded[1], 16)
                    w_loads.load(sp, n)
                sp.dma_start(x_loads.raw[0], x_loads.raw[1]).then_inc(x_loads.raw[2], 16)
            if out_rows is not None:
                with sp.Fori(0, CHUNKS) as c:
                    sp.wait_ge(y_added, c + 1)
                    sp.dma_start(out_rows[:, bass.ds(c * TPC, TPC), :],
                                 x[:, bass.ds(c * TPC, TPC), :]).then_inc(stored, 16)
                sp.wait_ge(stored, CHUNKS * 16)
            else:
                sp.wait_ge(y_added, CHUNKS)


def qkv_phase(nc, x, ident, w_raw, raw_loaded, bias_cols, bv_row, cos_t, sin_t, q_rows, k_rows, v, group_rows):
    N = 512
    B_T = x.shape[1] * P
    CHUNKS = B_T // N
    QM = 2
    UNITS = QM + 1
    _, KVH, _, HD = v.shape
    KV = KVH * HD

    with ExitStack() as ctx:
        def sb(name, shape, dt):
            return ctx.enter_context(nc.sbuf_tensor(f"qkv_{name}", shape, dt))

        def pb(name, shape, dt=F32):
            return ctx.enter_context(nc.psum_tensor(f"qkv_{name}", shape, dt))

        def sem(name):
            return ctx.enter_context(nc.semaphore(f"qkv_{name}"))

        normed = NormedChunks(nc, ctx, "qkv", x, ident, N, keep_all=True)
        TPC, KT = normed.TPC, normed.KT
        w_hi, w_lo = (sb(f"w_{n}", list(w_raw.shape), F32R) for n in ("hi", "lo"))
        biases = sb("biases", [P, 2 * UNITS], F32)
        bv = sb("bv", [P, KV], F32)
        cos = sb("cos", [P, B_T], F32)
        sin = sb("sin", [P, B_T], F32)
        by_cos = sb("by_cos", [P, UNITS, N], F32)
        by_sin = sb("by_sin", [P, UNITS, N], F32)
        turned = sb("turned", [P, UNITS, N], F32)
        rest = sb("rest", [P, UNITS, N], F32)
        parts = sb("parts", [P, UNITS, 3, N], BF16)
        qk_ps = [[pb(f"{w}{u}", [P, N]) for w in ("plain", "swapped")] for u in range(UNITS)]
        v_ps = normed.xt_ps[:, 0, :TPC * KV].rearrange("p (t c) -> p t c", t=TPC)

        tables_loaded = sem("tables_loaded")
        w_hi_ready = sem("w_hi_ready")
        w_lo_ready = sem("w_lo_ready")
        qk_done = sem("qk_done")
        v_done = sem("v_done")
        by_ready = sem("by_ready")
        turned_ready = sem("turned_ready")
        hi_ready = sem("hi_ready")
        rest_ready = sem("rest_ready")
        mid_ready = sem("mid_ready")
        lo_ready = sem("lo_ready")
        v_ready = sem("v_ready")
        PARTS = 3
        stored = group_rows.stored

        block = ctx.enter_context(nc.Block())

        @block.tensor
        def _(pe):
            def units(c, first=False, more=True):
                for u in range(UNITS):
                    if not first:
                        pe.wait_ge(by_ready, (c - 1) * UNITS + u + 1)
                    if u == UNITS - 1 and more:
                        pe.wait_ge(v_ready, c + 1)
                        normed.transpose(pe, c + 1)
                    for k in range(KT):
                        if u == 0:
                            normed.wait_split(pe, c, k)
                        for which in range(2):
                            col = (2 * u + which) * P
                            for n, (ws, xs) in enumerate(((w_hi, normed.xt_hi), (w_lo, normed.xt_hi), (w_hi, normed.xt_lo))):
                                last = pe.matmul(qk_ps[u][which][:], ws[:, k, col:col + P], xs[:, k, :],
                                                 start=(k == 0 and n == 0), stop=(k == KT - 1 and n == 2))
                        if k == 0 and u == UNITS - 1:
                            last.then_inc(normed.xt_used, 1)
                    last.then_inc(qk_done, 1)
                    if u == 0:
                        values(c)

            def values(c):
                col = 2 * UNITS * P
                for t in range(TPC):
                    rows = slice(t * P, (t + 1) * P)
                    n = 0
                    for k in range(KT):
                        for ws, xs in ((w_hi, normed.xt_hi), (w_lo, normed.xt_hi), (w_hi, normed.xt_lo)):
                            last = pe.matmul(v_ps[:, t, :], xs[:, k, rows], ws[:, k, col:col + KV],
                                             start=(n == 0 and t == 0), stop=(n == 3 * KT - 1), skip_group_check=True)
                            n += 1
                last.then_inc(v_done, 1)

            normed.transpose(pe, 0)
            pe.wait_ge(w_lo_ready, 1)
            units(0, first=True)
            with pe.Fori(1, CHUNKS - 1) as c:
                units(c)
            units(CHUNKS - 1, more=False)

        @block.scalar
        def _(act):
            def high(c, u):
                n = c * UNITS + u
                act.wait_ge(turned_ready, n + 1)
                act.wait_ge(stored[u][0], 16 * c)
                act.activation(parts[:, u, 0, :], turned[:, u, :], ACT.Copy).then_inc(hi_ready, 1)

            def mid(c, u):
                act.wait_ge(rest_ready, c * UNITS + u + 1)
                act.wait_ge(stored[u][1], 16 * c)
                act.activation(parts[:, u, 1, :], rest[:, u, :], ACT.Copy).then_inc(mid_ready, 1)

            def chunk(c, last=False):
                for u in range(UNITS):
                    high(c, u)
                    if u == UNITS - 2 and not last:
                        act.wait_ge(normed.xt_used, c + 1)
                        normed.high_parts(act, c + 1, 0)
                        act.wait_ge(qk_done, (c + 1) * UNITS)
                        for k in range(1, KT):
                            normed.high_parts(act, c + 1, k)
                    mid(c, u)

            act.wait_ge(raw_loaded, 16)
            act.activation(w_hi[:], w_raw, ACT.Copy).then_inc(w_hi_ready, 1)
            for k in range(KT):
                normed.high_parts(act, 0, k)
            with act.Fori(0, CHUNKS - 1) as c:
                chunk(c)
            chunk(CHUNKS - 1, last=True)

        @block.vector
        def _(dve):
            def turn(c, u):
                n = c * UNITS + u
                dve.wait_ge(qk_done, n + 1)
                tokens = bass.ds(c * N, N)
                dve.scalar_tensor_tensor(out=by_cos[:, u, :], in0=qk_ps[u][0][:], scalar=biases[:, 2 * u:2 * u + 1],
                                         in1=cos[:, tokens], op0=ALU.add, op1=ALU.mult)
                dve.scalar_tensor_tensor(out=by_sin[:, u, :], in0=qk_ps[u][1][:],
                                         scalar=biases[:, 2 * u + 1:2 * u + 2], in1=sin[:, tokens],
                                         op0=ALU.add, op1=ALU.mult).then_inc(by_ready, 1)

            def lo_part(c, u):
                dve.wait_ge(mid_ready, c * UNITS + u + 1)
                dve.wait_ge(stored[u][2], 16 * c)
                dve.tensor_tensor(parts[:, u, 2, :], rest[:, u, :], parts[:, u, 1, :], ALU.subtract).then_inc(lo_ready, 1)

            def values(c):
                dve.wait_ge(v_done, c + 1)
                for h in range(KVH):
                    cols = slice(h * HD, (h + 1) * HD)
                    last = dve.tensor_tensor(v[:, h, bass.ds(c * TPC, TPC), :], v_ps[:, :, cols],
                                             bv[:, None, cols].to_broadcast([P, TPC, HD]), ALU.add)
                last.then_inc(v_ready, 1)

            def chunk(c, first=False, last=False):
                turn(c, 0)
                if not first:
                    lo_part(c - 1, 2)
                if not last:
                    normed.normalise(dve, c + 1)
                turn(c, 1)
                values(c)
                if first:
                    for later in range(2, CHUNKS):
                        normed.statistics(dve, later)
                lo_part(c, 0)
                if not last:
                    for k in range(KT):
                        normed.low_parts(dve, c + 1, k)
                turn(c, 2)
                lo_part(c, 1)

            normed.statistics(dve, 0)
            dve.wait_ge(w_hi_ready, 1)
            dve.tensor_tensor(w_lo[:], w_raw, w_hi[:].bitcast(F32), ALU.subtract).then_inc(w_lo_ready, 1)
            normed.normalise(dve, 0)
            for k in range(KT):
                normed.low_parts(dve, 0, k)
            normed.statistics(dve, 1)
            dve.wait_ge(tables_loaded, 4 * 16)
            chunk(0, first=True)
            with dve.Fori(1, CHUNKS - 1) as c:
                chunk(c)
            chunk(CHUNKS - 1, last=True)
            lo_part(CHUNKS - 1, 2)

        @block.gpsimd
        def _(pool):
            def add_turned(c, u):
                pool.wait_ge(by_ready, c * UNITS + u + 1)
                pool.tensor_tensor(turned[:, u, :], by_cos[:, u, :], by_sin[:, u, :], ALU.add).then_inc(turned_ready, 1)

            def leave_rest(c, u):
                if u == 0:
                    pool.wait_ge(lo_ready, c * UNITS)
                pool.wait_ge(hi_ready, c * UNITS + u + 1)
                pool.tensor_tensor(rest[:, u, :], turned[:, u, :], parts[:, u, 0, :], ALU.subtract).then_inc(rest_ready, 1)

            def chunk(c):
                for u in range(UNITS):
                    add_turned(c, u)
                    leave_rest(c, u)

            normed.exponents(pool)
            normed.inverse_deviation(pool, 0)
            group_rows.fill_m(pool)
            normed.inverse_deviation(pool, 1)
            chunk(0)
            for c in range(2, CHUNKS):
                normed.inverse_deviation(pool, c)
            with pool.Fori(1, CHUNKS) as c:
                chunk(c)

        @block.sync
        def _(sp):
            sp.dma_start(biases[:], bias_cols).then_inc(tables_loaded, 16)
            sp.dma_start(bv[:], bv_row.partition_broadcast(P)).then_inc(tables_loaded, 16)
            sp.dma_start(cos[:], cos_t).then_inc(tables_loaded, 16)
            sp.dma_start(sin[:], sin_t).then_inc(tables_loaded, 16)

            def store(c):
                tokens = bass.ds(c * N, N)
                for u in range(UNITS):
                    for part, ready in enumerate((hi_ready, mid_ready, lo_ready)):
                        rows = (q_rows[u * P:(u + 1) * P, PARTS * part:PARTS * (part + 1), tokens] if u < QM
                                else k_rows[:, part::PARTS, tokens])
                        src = parts[:rows.shape[0], u, part, :]
                        sp.wait_ge(ready, c * UNITS + u + 1)
                        sp.dma_start(rows, src[:, None, :].to_broadcast([rows.shape[0], PARTS, N]))\
                          .then_inc(stored[u][part], 16)

            FIRST_BATCH = group_rows.T // N
            with sp.Fori(0, FIRST_BATCH) as c:
                store(c)
            group_rows.wait_stored(sp, FIRST_BATCH)
            sp.wait_ge(group_rows.filled, 2)
            group_rows.load_m(sp, 0, 0)
            with sp.Fori(FIRST_BATCH, CHUNKS) as c:
                store(c)
            group_rows.wait_stored(sp, CHUNKS)
            sp.wait_ge(v_ready, CHUNKS)


class GroupRows:

    LOADS = 2

    def __init__(self, nc, ctx, q_rows, k_rows, T, HD):
        HEADS, KVH = q_rows.shape[0] // HD, k_rows.shape[0] // HD
        self.T, self.QPK, self.ROWS = T, HEADS // KVH, q_rows.shape[1] * HD
        self.q_groups = q_rows.rearrange("(g i d) r t -> g (d r) i t", i=self.QPK, d=HD)
        self.k_groups = k_rows.rearrange("(g d) r t -> g (d r) t", d=HD)

        def sb(name, shape):
            return [ctx.enter_context(nc.sbuf_tensor(f"{name}{e}", shape, BF16)) for e in range(2)]

        self.mq, self.sq = sb("mq", [P, self.QPK, T]), sb("sq", [P, self.QPK, T])
        self.mk, self.sk = sb("mk", [P, T]), sb("sk", [P, T])
        self.filled = ctx.enter_context(nc.semaphore("rows_filled"))
        self.m_loaded = [ctx.enter_context(nc.semaphore(f"m_loaded{e}")) for e in range(2)]

        self.stored = [[ctx.enter_context(nc.semaphore(f"rows_stored{u}_{part}")) for part in range(3)] for u in range(3)]

    def wait_stored(self, sp, chunks):
        for sems in self.stored:
            for sem in sems:
                sp.wait_ge(sem, 16 * chunks)

    def fill_m(self, pool):
        self.zero(pool, (self.mq[0], self.mk[0], self.mq[1], self.mk[1]))

    def fill_s(self, pool):
        self.zero(pool, self.sq)
        for tile in self.sk:
            pool.memset(tile[:], -1.0).then_inc(self.filled, 1)

    def zero(self, pool, tiles):
        for tile in tiles:
            flat = tile[:].rearrange("p h t -> p (h t)") if len(tile.shape) == 3 else tile[:]
            pool.memset(flat.bitcast(F32), 0.0).then_inc(self.filled, 1)

    def load_m(self, sp, r, e):
        tokens = slice(e * self.T, (e + 1) * self.T)
        sp.dma_start(self.mq[e][:self.ROWS], self.q_groups[bass.ds(r, 1), :, :, tokens]
                     .rearrange("g r i t -> r (g i) t")).then_inc(self.m_loaded[e], 16)
        sp.dma_start(self.mk[e][:self.ROWS], self.k_groups[bass.ds(r, 1), :, tokens]
                     .rearrange("g r t -> r (g t)")).then_inc(self.m_loaded[e], 16)


def attention_phase(nc, group_rows, v, sum_tiles, sum_loads, wo_raw, wo_rows, wo_loaded, ident_bf, x, bo_row, T, HD):
    mq, mk, sq, sk, m_loaded = (group_rows.mq, group_rows.mk, group_rows.sq, group_rows.sk, group_rows.m_loaded)
    ROWS = group_rows.ROWS
    SHIFT = 2
    KVH = v.shape[1]
    B = x.shape[1] * P // T
    GROUPS = B * KVH
    QPK = group_rows.QPK
    KB = T // P
    N = 512
    QC = T // N
    TPC = N // P
    SCALE = 1.0 / float(HD) ** 0.5
    assert QPK == 4 and QC == 2 and GROUPS % 2 == 0 and ROWS + SHIFT <= P

    S_UNITS = []
    for qc in range(QC):
        full = [(kb, 0, N, 0) for kb in range(TPC * qc)]
        ends = [(TPC * qc + i, i * P, N - i * P, i * P) for i in range(TPC)]
        joined = (ends[3][0], ends[3][1], P, 0)
        S_UNITS += [(qc, [piece]) for piece in full + ends[:1]] + [(qc, [ends[1], joined]), (qc, [ends[2]])]
    SU = len(S_UNITS)
    SPAN = [slice(min(at for *_, at in pieces), N) for _, pieces in S_UNITS]
    MASKS = [[at for kb, _, _, at in pieces if kb >= TPC * qc] for qc, pieces in S_UNITS]
    DIAGONAL = [u for u in range(SU) if MASKS[u]]
    CHUNK_FIRST = [[q for q, _ in S_UNITS].index(qc) for qc in range(QC)]
    CHUNK_LAST = [first - 1 for first in CHUNK_FIRST[1:]] + [SU - 1]
    M_UNITS = [(t, h, kc, min(N, (t + 1) * P - kc * N)) for t in range(KB) for kc in range(t // TPC + 1)
               for h in range(QPK)]
    MU = len(M_UNITS)
    MU_HALF = TPC * QPK
    halves = [sorted(half, key=lambda unit: -unit[3]) for half in (M_UNITS[:MU_HALF], M_UNITS[MU_HALF:])]
    M_UNITS = [half.pop(-(i % 2)) for half in halves for i in range(len(half))]

    AHEAD = 2
    LEAD = 3
    M_BANKS = 4
    S_BANKS = 3
    SHARES = (0.3, 0.18, 0.18, 0.18, 0.16)
    width = [sum(w for _, _, w, _ in pieces) for _, pieces in S_UNITS]
    work = [width[u] + width[(u + AHEAD) % SU] for u in range(SU)]
    m_cost = [n + 80 for *_, n in M_UNITS]
    PLACES = [[[] for _ in SHARES] for _ in range(SU)]
    ITEMS = []
    order = [*range(SU - LEAD, SU), *range(SU - LEAD)]
    done = upto = unit = 0
    turn_first = None
    for u in order:
        ahead = 1 + (u >= SU - LEAD)
        if turn_first is None and unit > MU_HALF:
            turn_first = u
        for slot, share in enumerate(SHARES):
            upto += work[u] * share
            while unit < MU and (done < sum(m_cost) * upto / sum(work) or (u, slot) == (order[-1], QPK)):
                done += m_cost[unit]
                PLACES[u][slot].append((ahead, len(ITEMS)))
                ITEMS.append(("max", unit))
                unit += 1
        if u == SU - LEAD + 1 or u == turn_first:
            PLACES[u][-1].append((ahead, len(ITEMS)))
            ITEMS.append(("turn", int(u != turn_first)))
    FIRST_ITEMS = sum(len(slot) for u in order[:LEAD] for slot in PLACES[u])
    PERIOD = -(-len(ITEMS) // M_BANKS) * M_BANKS
    TURN_AT = [turn_first, SU - LEAD + 1]
    assert turn_first < SU - LEAD and ITEMS.index(("turn", 1)) < ITEMS.index(("turn", 0))

    S_PERIOD = -(-SU * QPK // S_BANKS) * S_BANKS

    def s_user(i):
        i -= S_BANKS
        while i < 0 and i + S_PERIOD >= SU * QPK:
            i -= S_BANKS
        return i if i >= 0 else i + S_PERIOD - SU * QPK

    def bank_user(g, i):
        while True:
            i -= M_BANKS
            if i < 0:
                i += PERIOD
                g = g - 1
            if i < len(ITEMS):
                kind, number = ITEMS[i]
                return (kind, g * MU + number + 1 if kind == "max" else QC * g + 1 - number)

    with ExitStack() as ctx:
        def sb(name, shape, dt):
            return ctx.enter_context(nc.sbuf_tensor(f"att_{name}", shape, dt))

        def pb(name, shape, dt=F32):
            return ctx.enter_context(nc.psum_tensor(f"att_{name}", shape, dt))

        def sem(name):
            return ctx.enter_context(nc.semaphore(f"att_{name}"))

        vs = [sb(f"vs{e}", [P, KB, 32], F32) for e in range(2)]
        probs = [sb(f"probs{i}", [P, QPK, N], F32) for i in range(5)]
        causal = sb("causal", [P, N], F32)
        scratch = [sb(f"scratch{i}", [P, N], BF16) for i in range(M_BANKS)]
        maxima = sb("maxima", [P, QPK, KB, QC], F32)
        top = sb("top", [P, TPC, QPK], F32)
        shift = [sb(f"shift{i}", [P, TPC, QPK, SHIFT], BF16) for i in range(QC)]
        shift_t = [sb(f"shift_t{i}", [QPK * SHIFT, N], BF16) for i in range(QC)]
        sums = [sb(f"sums{qc}", [P, N], F32) for qc in range(QC)]
        bo = sb("bo", [P, x.shape[2]], F32)

        s_ps = [pb(f"s_ps{i}", [P, N]) for i in range(S_BANKS)]
        m_ps = [pb(f"m_ps{i}", [P, N]) for i in range(M_BANKS)]
        o_ps = pb("o_ps", [P, N])
        t_ps = [ps[:QPK * SHIFT, :N // 2].bitcast(BF16) for ps in m_ps]

        masks_ready = sem("masks_ready")
        ones_ready = sem("ones_ready")
        s_loaded = [sem(f"s_loaded{e}") for e in range(2)]
        shift_loaded = [sem(f"shift_loaded{i}") for i in range(QC)]
        bo_loaded = sem("bo_loaded")
        v_staged = sem("v_staged")
        m_done = sem("m_done")
        m_taken = sem("m_taken")
        top_ready = sem("top_ready")
        shift_ready = sem("shift_ready")
        t_done = sem("t_done")
        shift_t_ready = sem("shift_t_ready")
        s_done = sem("s_done")
        exp_done = sem("exp_done")
        masked = sem("masked")
        pv_done = sem("pv_done")
        o_taken = sem("o_taken")
        sums_stored = [[sem(f"sums_stored{e}_{qc}") for qc in range(QC)] for e in range(2)]
        passed = sem("passed")
        x_biased = sem("x_biased")

        block = ctx.enter_context(nc.Block())

        def after(r, e):
            return (r, 1) if e == 0 else (r + 1, 0)

        ROUNDS = GROUPS // 2

        @block.tensor
        def _(pe):
            def wait_bank(g, i):
                kind, count = bank_user(g, i)
                if isinstance(count, int):
                    if kind == "max":
                        count = min(count, GROUPS * MU)
                    if count <= 0:
                        return
                pe.wait_ge(m_taken if kind == "max" else shift_t_ready, count)

            def m_item(r, e, i):
                g = 2 * r + e
                kind, number = ITEMS[i]
                bank = i % M_BANKS
                if kind == "turn":
                    if isinstance(g, int) and g == 0 and number:
                        return
                    pe.wait_ge(shift_ready, QC * g + 1 - number)
                    wait_bank(g, i)
                    for t in range(TPC):
                        last = pe.transpose(t_ps[bank][:, t * P:(t + 1) * P],
                                            shift[number][:, t, :, :].rearrange("p h s -> p (h s)"), ident_bf[:])
                    last.then_inc(t_done, 1)
                elif not (isinstance(g, int) and g == GROUPS):
                    t, h, kc, n = M_UNITS[number]
                    if number == 0:
                        pe.wait_ge(m_loaded[e], 16 * 2 * (r + 1))
                    wait_bank(g, i)
                    pe.matmul(m_ps[bank][:, :n], mq[e][:, h, t * P:(t + 1) * P], mk[e][:, kc * N:kc * N + n],
                              start=True, stop=True).then_inc(m_done, 1)

            def s_head(r, e, u, h):
                g = 2 * r + e
                n = g * SU + u
                qc, pieces = S_UNITS[u]
                if h == 0 and u == 0:
                    pe.wait_ge(s_loaded[e], 16 * 2 * (r + 1))
                if h == 0 and u in CHUNK_FIRST:
                    pe.wait_ge(shift_loaded[qc], 16 * QPK * (g + 1))
                before = s_user(u * QPK + h)
                if not (isinstance(g, int) and g == 0 and before < 0):
                    pe.wait_ge(exp_done, n * QPK + before - u * QPK + 1)
                for kb, q0, w, at in pieces:
                    last = pe.matmul(s_ps[(u * QPK + h) % S_BANKS][:, at:at + w], sk[e][:, kb * P:(kb + 1) * P],
                                     sq[e][:, h, qc * N + q0:qc * N + q0 + w], start=True, stop=True)
                last.then_inc(s_done, 1)

            def value_unit(r, e, u):
                g = 2 * r + e
                qc, pieces = S_UNITS[u]
                n = g * SU + u
                if u == 0:
                    pe.wait_ge(v_staged, g + 1)
                if u in CHUNK_FIRST:
                    pe.wait_ge(o_taken, QC * g + qc)
                pe.wait_ge(exp_done, QPK * (n + 1))
                if u in DIAGONAL:
                    pe.wait_ge(masked, g * sum(map(len, MASKS)) + sum(map(len, MASKS[:u + 1])))
                for kb, q0, w, at in pieces:
                    for h in range(QPK):
                        last = pe.matmul(o_ps[32 * h:32 * (h + 1), q0:q0 + w], vs[e][:, kb, :],
                                         probs[u % len(probs)][:, h, at:at + w],
                                         start=(u in CHUNK_FIRST), stop=(u in CHUNK_LAST))
                last.then_inc(pv_done, 1)

            def group(r, e, groups_left=GROUPS):
                r1, e1 = after(r, e)
                for u in range(SU):
                    for slot in range(QPK + 1):
                        if slot == QPK:
                            value_unit(r, e, u)
                        elif u + AHEAD < SU:
                            s_head(r, e, u + AHEAD, slot)
                        elif groups_left:
                            s_head(r1, e1, u + AHEAD - SU, slot)
                        for ahead, i in PLACES[u][slot]:
                            if groups_left and ahead <= groups_left + 1:
                                m_item(*((r1, e1) if ahead == 1 else (r + 1, e)), i)

            pe.sem_inc(pv_done, len(probs))
            for i in range(len(ITEMS)):
                m_item(0, 0, i)
            for i in range(FIRST_ITEMS):
                m_item(0, 1, i)
            for u in range(AHEAD):
                for h in range(QPK):
                    s_head(0, 0, u, h)
            with pe.Fori(0, ROUNDS - 1) as r:
                group(r, 0)
                group(r, 1)
            group(ROUNDS - 1, 0, groups_left=1)
            group(ROUNDS - 1, 1, groups_left=0)

        @block.vector
        def _(dve):
            def m_unit(r, e, m):
                t, h, kc, n = M_UNITS[m]
                bank = ITEMS.index(("max", m)) % M_BANKS
                top_of = maxima[:, h, t, kc:kc + 1]
                wait_apart(dve, m_done, (2 * r + e) * MU + m + 1, passed)
                if kc == t // TPC:
                    dve.tensor_tensor_reduce(out=scratch[bank][:, :n], in0=m_ps[bank][:, :n], in1=causal[:, N - n:], scale=1.0,
                                             scalar=LOWEST, op0=ALU.add, op1=ALU.max, accum_out=top_of).then_inc(m_taken, 1)
                else:
                    dve.tensor_reduce(top_of, m_ps[bank][:, :n], mybir.AxisListType.X, ALU.max).then_inc(m_taken, 1)

            def join_maxima(r, e, qc):
                g = 2 * r + e
                dve.wait_ge(m_taken, g * MU + (MU if qc else MU_HALF))
                dve.wait_ge(shift_ready, QC * g + qc)
                blocks = maxima[:, :, qc * TPC:(qc + 1) * TPC, :].rearrange("p h t k -> p t h k")
                for out in (shift[qc][:, :, :, 0], top[:]):
                    dve.tensor_reduce(out, blocks, mybir.AxisListType.X, ALU.max).then_inc(top_ready, 1)

            def group(r, e):
                for m in range(MU):
                    m_unit(r, e, m)
                    if m == MU_HALF + 1:
                        join_maxima(r, e, 0)
                join_maxima(r, e, 1)

            dve.memset(maxima[:], LOWEST).then_inc(passed, 1)
            dve.wait_ge(passed, 1)
            dve.wait_ge(masks_ready, 2)
            with dve.Fori(0, ROUNDS) as r:
                group(r, 0)
                group(r, 1)

        @block.scalar
        def _(act):
            def exponentials(r, e, u, h):
                n = (2 * r + e) * SU + u
                if h == 0:
                    act.wait_ge(pv_done, n + 1)
                act.wait_ge(s_done, QPK * n + h + 1)
                act.activation(probs[u % len(probs)][:, h, SPAN[u]], s_ps[(u * QPK + h) % S_BANKS][:, SPAN[u]], ACT.Exp,
                               scale=SCALE).then_inc(exp_done, 1)

            def take_shift(r, e, qc):
                g = 2 * r + e
                act.wait_ge(t_done, QC * g + qc + 1)
                act.wait_ge(shift_loaded[qc], 16 * QPK * g)
                bank = ITEMS.index(("turn", qc)) % M_BANKS
                act.activation(shift_t[qc][:], t_ps[bank], ACT.Copy).then_inc(shift_t_ready, 1)

            def take_sums(r, e, qc):
                g = 2 * r + e
                act.wait_ge(pv_done, g * SU + CHUNK_LAST[qc] + 1 + len(probs))
                if e:
                    act.wait_ge(sums_stored[0][qc], 16 * QPK * (r + 1))
                else:
                    act.wait_ge(sums_stored[1][qc], 16 * QPK * r)
                act.activation(sums[qc][:], o_ps[:], ACT.Copy).then_inc(o_taken, 1)

            def chunk_end(r, e, u):
                if u in CHUNK_LAST:
                    take_sums(r, e, CHUNK_LAST.index(u))

            def group(r, e, last=False):
                r1, e1 = after(r, e)
                for u in range(SU):
                    for h in range(QPK):
                        if u + AHEAD < SU:
                            exponentials(r, e, u + AHEAD, h)
                        elif not last:
                            exponentials(r1, e1, u + AHEAD - SU, h)
                        if h == 0 and u:
                            chunk_end(r, e, u - 1)
                        elif h == 0:
                            before_end(r, e)
                    if u in TURN_AT and not last:
                        take_shift(r1, e1, TURN_AT.index(u))
                if last:
                    chunk_end(r, e, SU - 1)

            def before_end(r, e):
                if e == 1:
                    chunk_end(r, 0, SU - 1)
                elif not (isinstance(r, int) and r == 0):
                    chunk_end(r - 1, 1, SU - 1)

            for qc in range(QC):
                take_shift(0, 0, qc)
            for u in range(AHEAD):
                for h in range(QPK):
                    exponentials(0, 0, u, h)
            group(0, 0)
            group(0, 1)
            with act.Fori(1, ROUNDS - 1) as r:
                group(r, 0)
                group(r, 1)
            group(ROUNDS - 1, 0)
            group(ROUNDS - 1, 1, last=True)

        @block.gpsimd
        def _(pool):
            def mask(r, e, u):
                g = 2 * r + e
                wait_apart(pool, exp_done, QPK * (g * SU + u + 1), passed)
                for at in MASKS[u]:
                    blk = probs[u % len(probs)][:, :, at:at + P]
                    pool.affine_select(out=blk, in_=blk, compare_op=ALU.is_ge, fill=0.0, base=0,
                                       pattern=[[0, QPK], [1, P]], channel_multiplier=-1).then_inc(masked, 1)

            def stage_values(r, e):
                g = 2 * r + e
                pool.tensor_copy(vs[e][:, :, 0:HD], v.rearrange("p h (b k) d -> p (h b k) d", b=B)
                                 [:, bass.ds(g * KB, KB), :]).then_inc(v_staged, 1)

            def add_bias(r, e):
                tile = x[:, bass.ds(2 * r + e, 1), :].rearrange("p a c -> p (a c)")
                pool.tensor_tensor(tile, tile, bo[:], ALU.add).then_inc(x_biased, 1)

            SPLIT_AFTER = (CHUNK_LAST[0], SU - 2)

            def split_maxima(r, e, qc):
                g = 2 * r + e
                pool.wait_ge(top_ready, 2 * (QC * g + qc + 1))
                pool.tensor_tensor(shift[qc][:, :, :, 1], top[:], shift[qc][:, :, :, 0], ALU.subtract)\
                    .then_inc(shift_ready, 1)

            def group(r, e, last=False):
                if not last:
                    pool.wait_ge(pv_done, (2 * r + e) * SU + len(probs))
                    stage_values(*after(r, e))
                for u in DIAGONAL:
                    mask(r, e, u)
                    if u in SPLIT_AFTER and not last:
                        split_maxima(*after(r, e), SPLIT_AFTER.index(u))
                    if u == CHUNK_LAST[0]:
                        add_bias(r, e)

            pool.memset(causal[:], 0.0).then_inc(masks_ready, 1)
            pool.wait_ge(masks_ready, 1)
            pool.affine_select(out=causal[:, N - P:], in_=causal[:, N - P:], compare_op=ALU.is_ge, fill=MASKED, base=0,
                               pattern=[[-1, P]], channel_multiplier=1).then_inc(masks_ready, 1)
            group_rows.fill_s(pool)
            for e in range(2):
                pool.memset(vs[e][:], 0.0).then_inc(ones_ready, 1)
            pool.wait_ge(ones_ready, 2)
            for e in range(2):
                pool.memset(vs[e][:, :, HD:HD + 1], 1.0).then_inc(ones_ready, 1)
            pool.wait_ge(ones_ready, 4)
            stage_values(0, 0)
            for qc in range(QC):
                split_maxima(0, 0, qc)
            pool.wait_ge(bo_loaded, 16)
            with pool.Fori(0, ROUNDS - 1) as r:
                group(r, 0)
                group(r, 1)
            group(ROUNDS - 1, 0)
            group(ROUNDS - 1, 1, last=True)

        @block.sync
        def _(sp):
            LOADS = group_rows.LOADS
            load_m = group_rows.load_m

            def copy_s(r, e):
                sp.wait_ge(m_loaded[e], 16 * LOADS * (r + 1))
                sp.dma_start(sq[e][:ROWS], mq[e][:ROWS]).then_inc(s_loaded[e], 16)
                sp.dma_start(sk[e][:ROWS], mk[e][:ROWS]).then_inc(s_loaded[e], 16)

            def load_shift(r, e, qc):
                sp.wait_ge(shift_t_ready, QC * (2 * r + e) + qc + 1)
                for h in range(QPK):
                    sp.dma_start(sq[e][ROWS:ROWS + SHIFT, h, qc * N:(qc + 1) * N],
                                 shift_t[qc][h * SHIFT:(h + 1) * SHIFT, :]).then_inc(shift_loaded[qc], 16)

            def store_sums(r, e, qc):
                sp.wait_ge(o_taken, QC * (2 * r + e) + qc + 1)
                tile = e * KB + qc * TPC
                rows = sum_tiles[tile:tile + TPC].rearrange("t (g h c) n -> t g h c n", h=QPK, c=HD + 1)
                for h in range(QPK):
                    sp.dma_start(rows[:, bass.ds(r, 1), h].rearrange("t g c n -> (g c) t n"),
                                  sums[qc][32 * h:32 * h + HD + 1].rearrange("p (t n) -> p t n", n=P))\
                       .then_inc(sums_stored[e][qc], 16)

            def next_m(r, e):
                sp.wait_ge(s_loaded[e], 16 * LOADS * (r + 1))
                sp.wait_ge(m_done, MU * (2 * r + e + 1))
                load_m(sp, r + 1, e)

            def group(r, e, loads=True, last=False):
                r1, e1 = after(r, e)
                if not last:
                    sp.wait_ge(s_done, QPK * SU * (2 * r + e))
                    copy_s(r1, e1)
                    load_shift(r1, e1, 0)
                store_sums(r, e, 0)
                if not last:
                    load_shift(r1, e1, 1)
                if loads:
                    next_m(r1, e1)
                store_sums(r, e, 1)

            sp.dma_start(bo[:], bo_row.partition_broadcast(P)).then_inc(bo_loaded, 16)
            load_m(sp, 0, 1)
            sp.wait_ge(group_rows.filled, 8)
            copy_s(0, 0)
            load_shift(0, 0, 0)
            load_shift(0, 0, 1)
            next_m(0, 0)
            with sp.Fori(0, ROUNDS - 2) as r:
                group(r, 0)
                group(r, 1)
            group(ROUNDS - 2, 0)
            group(ROUNDS - 2, 1, loads=False)
            group(ROUNDS - 1, 0, loads=False)
            group(ROUNDS - 1, 1, loads=False, last=True)
            sp.dma_start(wo_raw[:], wo_rows).then_inc(wo_loaded, 16)
            for qc in range(QC):
                sp.wait_ge(sums_stored[0][qc], 16 * QPK * ROUNDS)
            for e in range(2):
                sum_loads.load(sp, 0, e)
            for qc in range(QC):
                sp.wait_ge(sums_stored[1][qc], 16 * QPK * ROUNDS)
            sp.wait_ge(x_biased, GROUPS)


class SumLoads:

    BLOCKS = 3

    def __init__(self, nc, ctx, sum_tiles):
        self.rows = sum_tiles.rearrange("a (b p) n -> a p b n", b=self.BLOCKS)
        self.ROWS = self.rows.shape[1]
        assert self.ROWS <= P
        self.sums = [ctx.enter_context(nc.sbuf_tensor(f"tile_sums{e}", [self.ROWS, self.BLOCKS, P], F32)) for e in range(2)]
        self.loaded = [ctx.enter_context(nc.semaphore(f"tile_sums_loaded{e}")) for e in range(2)]

    def load(self, sp, r, e):
        sp.dma_start(self.sums[e][:], self.rows[bass.ds(2 * r + e, 1)].rearrange("a p b n -> p (a b) n"))\
          .then_inc(self.loaded[e], 16)


def output_phase(nc, sum_loads, wo_raw, wo_loaded, ident, x, HD):
    _, TILES, C = x.shape
    KT = C // P
    HEADS = C // HD
    ROWS, BLOCKS, sums, loaded = sum_loads.ROWS, sum_loads.BLOCKS, sum_loads.sums, sum_loads.loaded
    with ExitStack() as ctx:
        def sb(name, shape, dt):
            return [ctx.enter_context(nc.sbuf_tensor(f"out_{name}{e}", shape, dt)) for e in range(2)]

        def pb(name, shape):
            return [ctx.enter_context(nc.psum_tensor(f"out_{name}{e}", shape, F32)) for e in range(2)]

        def sem(name):
            return ctx.enter_context(nc.semaphore(f"out_{name}"))

        wo = [ctx.enter_context(nc.sbuf_tensor(f"wo_{n}", [P, KT, C], F32R)) for n in ("hi", "lo")]
        inverse = sb("inverse", [P, HEADS, 1], F32)
        attn = sb("attn", [P, HEADS, HD], F32)
        at_hi = sb("at_hi", [P, KT, P], F32R)
        at_lo = sb("at_lo", [P, KT, P], F32R)
        sums_ps = pb("sums_ps", [P, BLOCKS * ROWS])
        at_ps = pb("at_ps", [P, KT, P])
        y_ps = pb("y_ps", [P, C])

        sums_done = sem("sums_done")
        inverse_ready = sem("inverse_ready")
        attn_ready = sem("attn_ready")
        at_done = sem("at_done")
        hi_ready = sem("hi_ready")
        lo_ready = sem("lo_ready")
        y_done = sem("y_done")
        y_added = sem("y_added")
        wo_hi_ready = sem("wo_hi_ready")
        wo_lo_ready = sem("wo_lo_ready")
        block = ctx.enter_context(nc.Block())
        ROUNDS = TILES // 2

        def skewed(engine, steps):
            S = len(steps) - 1
            FIRST = (S + 3) // 2

            def tile(r, n, low=0, high=len(steps)):
                for k in range(low, high):
                    steps[k](r + (n - k) // 2, (n - k) % 2)

            for n in range(2 * FIRST):
                tile(0, n, high=min(n, S) + 1)
            with engine.Fori(FIRST, ROUNDS) as r:
                tile(r, 0)
                tile(r, 1)
            for n in range(S):
                tile(ROUNDS, n, low=n + 1)

        def before(engine, signal, r, e):
            if not (isinstance(r, int) and r < 1):
                engine.wait_ge(signal, 2 * r + e - 1)

        @block.sync
        def _(sp):
            with sp.Fori(1, ROUNDS) as r:
                for e in range(2):
                    sp.wait_ge(sums_done, 2 * r + e - 1)
                    sum_loads.load(sp, r, e)
            sp.wait_ge(y_added, TILES)

        @block.tensor
        def _(pe):
            def transpose_sums(r, e):
                pe.wait_ge(loaded[e], 16 * (r + 1))
                before(pe, attn_ready, r, e)
                for b in range(BLOCKS):
                    last = pe.transpose(sums_ps[e][:, b * ROWS:(b + 1) * ROWS], sums[e][:, b, :], ident[:ROWS, :ROWS])
                last.then_inc(sums_done, 1)

            def transpose_attn(r, e):
                pe.wait_ge(attn_ready, 2 * r + e + 1)
                before(pe, lo_ready, r, e)
                flat = attn[e][:].rearrange("p h d -> p (h d)")
                for k in range(KT):
                    last = pe.transpose(at_ps[e][:, k, :], flat[:, k * P:(k + 1) * P], ident[:])
                last.then_inc(at_done, 1)

            def project(r, e):
                if isinstance(r, int) and (r, e) == (0, 0):
                    pe.wait_ge(wo_lo_ready, 1)
                pe.wait_ge(hi_ready, 2 * r + e + 1)
                pe.wait_ge(lo_ready, 2 * r + e + 1)
                before(pe, y_added, r, e)
                i = 0
                for k in range(KT):
                    for hs, ws in ((at_hi[e], wo[0]), (at_hi[e], wo[1]), (at_lo[e], wo[0])):
                        last = pe.matmul(y_ps[e][:], hs[:, k, :], ws[:, k, :], start=(i == 0), stop=(i == 3 * KT - 1))
                        i += 1
                last.then_inc(y_done, 1)

            skewed(pe, [transpose_sums, transpose_attn, project])

        @block.scalar
        def _(act):
            def high_part(r, e):
                act.wait_ge(at_done, 2 * r + e + 1)
                before(act, y_done, r, e)
                act.activation(at_hi[e][:], at_ps[e][:], ACT.Copy).then_inc(hi_ready, 1)

            act.wait_ge(wo_loaded, 16)
            act.activation(wo[0][:], wo_raw[:], ACT.Copy).then_inc(wo_hi_ready, 1)
            skewed(act, [high_part])

        @block.vector
        def _(dve):
            def divide(r, e):
                dve.wait_ge(sums_done, 2 * r + e + 1)
                before(dve, at_done, r, e)
                rows = sums_ps[e][:].rearrange("p (h d) -> p h d", h=HEADS)
                dve.reciprocal(inverse[e][:], rows[:, :, HD:HD + 1]).then_inc(inverse_ready, 1)
                dve.wait_ge(inverse_ready, 2 * r + e + 1)
                dve.tensor_tensor(attn[e][:], rows[:, :, 0:HD], inverse[e][:].to_broadcast([P, HEADS, HD]),
                                  ALU.mult).then_inc(attn_ready, 1)

            def low_part(r, e):
                dve.wait_ge(hi_ready, 2 * r + e + 1)
                dve.tensor_tensor(at_lo[e][:], at_ps[e][:], at_hi[e][:].bitcast(F32), ALU.subtract).then_inc(lo_ready, 1)

            def add(r, e):
                dve.wait_ge(y_done, 2 * r + e + 1)
                tile = x[:, bass.ds(2 * r + e, 1), :].rearrange("p a c -> p (a c)")
                dve.tensor_tensor(tile, y_ps[e][:], tile, ALU.add).then_inc(y_added, 1)

            dve.wait_ge(wo_hi_ready, 1)
            dve.tensor_tensor(wo[1][:], wo_raw[:], wo[0][:].bitcast(F32), ALU.subtract).then_inc(wo_lo_ready, 1)
            skewed(dve, [divide, low_part, add])


def build(nc, x_in, w_qkv, bias_cols, bv, w_o, bo, w_gate, w_up, w_down, cos_t, sin_t, out, HD=8, SPLIT=9):
    B, T, C = x_in.shape
    TILES = B * T // P
    HID = w_gate.shape[1]
    KT, BLKS, J = C // P, HID // 512, 4
    FIRST = 512 // P
    KV = bv.shape[0]
    KVH = KV // HD
    with ExitStack() as ctx:
        def sb(name, shape, dt, on=ctx):
            return on.enter_context(nc.sbuf_tensor(name, shape, dt))

        x = sb("x", [P, TILES, C], F32)
        ident = sb("ident", [P, P], F32)
        ident_bf = sb("ident_bf", [P, P], BF16)
        parts = ("hi", "lo")
        wg = [sb(f"wg_{n}", [P, KT, BLKS, J, P], F32R) for n in parts]
        wu = [sb(f"wu_{n}", [P, KT, BLKS, J, P], F32R) for n in parts]
        wd = [sb(f"wd_{n}", [P, BLKS, J, C], F32R) for n in parts]
        x_rows = x_in.rearrange("b (t p) c -> p (b t) c", p=P)
        out_rows = out.rearrange("b (t p) c -> p (b t) c", p=P)
        q_rows = nc.dram_tensor("q_rows", [C, SPLIT, B * T], BF16).ap()
        k_rows = nc.dram_tensor("k_rows", [KV, SPLIT, B * T], BF16).ap()
        sum_tiles = nc.dram_tensor("sum_tiles", [TILES, C // HD * (HD + 1), P], F32).ap()

        qkv_raw_loaded = ctx.enter_context(nc.semaphore("qkv_raw_loaded"))
        until_qkv = ctx.enter_context(ExitStack())
        qkv_raw = sb("qkv_raw", [P, KT, w_qkv.shape[1]], F32, until_qkv)
        with ExitStack() as in_ffn1:
            raw_g, raw_u = (sb(f"raw_{n}", [P, BLKS, KT, 512], F32, in_ffn1) for n in ("g", "u"))
            raw_d = sb("raw_d", [P, BLKS, J, C], F32, in_ffn1)
            loads = []
            for b in range(BLKS):
                for w, raw, (hi, lo) in ((w_gate, raw_g, wg), (w_up, raw_u, wu)):
                    loads.append((w.rearrange("(k p) n -> p k n", p=P)[:, :, b * 512:(b + 1) * 512], raw[:, b],
                                  raw[:, b].rearrange("p k (q j) -> p k j q", j=J), hi[:, :, b], lo[:, :, b]))
            for b in range(BLKS):
                loads.append((w_down.rearrange("(b p j) c -> p b j c", p=P, j=J)[:, b], raw_d[:, b], raw_d[:, b],
                              wd[0][:, b], wd[1][:, b]))
            x_loads = XLoads([(x[:, :FIRST], x_rows[:, :FIRST]), (x[:, FIRST:], x_rows[:, FIRST:])],
                             ctx.enter_context(nc.semaphore("ident_ready")), ident_bf,
                             (qkv_raw[:], w_qkv.rearrange("(k p) n -> p k n", p=P), qkv_raw_loaded))
            ffn_phase(nc, "ffn1", x, (wg, wu, wd), ident, first_loads=(x_loads, WeightLoads(nc, ctx, "ffn1", loads)))
        until_output = ctx.enter_context(ExitStack())
        sum_loads = SumLoads(nc, until_output, sum_tiles)
        wo_raw = sb("wo_raw", [P, KT, C], F32, until_output)
        wo_loaded = ctx.enter_context(nc.semaphore("wo_loaded"))
        until_attention = ctx.enter_context(ExitStack())
        v = sb("v", [P, KVH, TILES, HD], F32, until_attention)
        group_rows = GroupRows(nc, until_attention, q_rows, k_rows, T, HD)
        qkv_phase(nc, x, ident, qkv_raw[:], qkv_raw_loaded, bias_cols, bv, cos_t, sin_t, q_rows, k_rows, v, group_rows)
        attention_phase(nc, group_rows, v, sum_tiles, sum_loads, wo_raw, w_o.rearrange("(k p) n -> p k n", p=P), wo_loaded,
                        ident_bf, x, bo, T, HD)
        until_attention.close()
        output_phase(nc, sum_loads, wo_raw, wo_loaded, ident, x, HD)
        until_output.close()
        ffn_phase(nc, "ffn2", x, (wg, wu, wd), ident, out_rows=out_rows)


def rope_tables(T, B, HD):
    import numpy as np

    inverse = (1.0 / np.float32(ROPE_BASE) ** (np.arange(0, HD, 2, dtype=np.float32) / np.float32(HD))).astype(np.float32)
    angles = np.outer(np.arange(T, dtype=np.float32), inverse).astype(np.float32)
    cos = np.repeat(np.cos(angles), 2, axis=1).T
    sin = np.repeat(np.sin(angles), 2, axis=1).T * np.tile(np.array([[-1.0], [1.0]], np.float32), (HD // 2, 1))
    return (np.ascontiguousarray(np.tile(cos, (P // HD, B)), dtype=np.float32),
            np.ascontiguousarray(np.tile(sin, (P // HD, B)), dtype=np.float32))


def swapped(a):
    return a.reshape(*a.shape[:-1], -1, 2)[..., ::-1].reshape(a.shape)


def kernel(**inputs):
    import numpy as np
    import concourse.bacc as bacc
    from concourse.bass_utils import run_bass_kernel_spmd

    a = {name.split("_", 1)[1]: np.asarray(value) for name, value in inputs.items()}
    x = a["attn_x"]
    B, T, C = x.shape
    HD = 8
    wq, wk, bq, bk = a["attn_Wq"], a["attn_Wk"], a["attn_bq"], a["attn_bk"]
    tiles = [wq[:, :P], wq[:, P:], np.concatenate([wk, wk], axis=1)]
    w_qkv = np.concatenate([w for t in tiles for w in (t, swapped(t))] + [a["attn_Wv"]], axis=1)
    b_tiles = [bq[:P], bq[P:], np.concatenate([bk, bk])]
    bias_cols = np.stack([b for t in b_tiles for b in (t, swapped(t))], axis=1)
    cos_t, sin_t = rope_tables(T, B, HD)
    arrays = {"x": x, "w_qkv": w_qkv, "bias_cols": bias_cols, "bv": a["attn_bv"], "w_o": a["attn_Wo"], "bo": a["attn_bo"],
              "w_gate": a["ffn_w_gate"], "w_up": a["ffn_w_up"], "w_down": a["ffn_w_down"], "cos_t": cos_t, "sin_t": sin_t}
    nc = bacc.Bacc("TRN2", target_bir_lowering=False, num_devices=1)
    arrays = {f"in_{name}": np.ascontiguousarray(value) for name, value in arrays.items()}
    args = [nc.dram_tensor(name, value.shape, mybir.dt.from_np(value.dtype), kind="ExternalInput").ap()
            for name, value in arrays.items()]
    out = nc.dram_tensor("out", x.shape, F32, kind="ExternalOutput").ap()
    build(nc, *args, out)
    result = run_bass_kernel_spmd(nc, [arrays], core_ids=[0])
    return result.results[0]["out"]
```
